# Optimizing a Trainium2 kernel written in Bass

```python
import numpy as np
import jax
import jax.numpy as jnp

def _softmax(x, axis=-1):
    return jax.nn.softmax(x, axis=axis)

def _gelu(x):
    return jax.nn.gelu(x, approximate=True)

def _silu(x):
    return jax.nn.silu(x)

def _sigmoid(x):
    return jax.nn.sigmoid(x)

def _layernorm(x, axis=-1, eps=1e-05):
    m = jnp.mean(x, axis=axis, keepdims=True)
    v = jnp.var(x, axis=axis, keepdims=True)
    return (x - m) / jnp.sqrt(v + eps)

def _scatter_add(tgt, idx, src, axis=0):
    return tgt.at[idx].add(src)

def _segment_sum(src, seg, n):
    return jax.ops.segment_sum(src, seg, n)
kernel_name = 'mk_seq_postln_d1_jaxref_r8_890d24'

def setup_inputs(seed: int=0):
    np.random.seed(seed)
    _w = jnp.asarray

    def _L0_attn_setup():
        import jax, jax.numpy as jnp
        import numpy as np
        B, S, HID = (2, 256, 256)
        NH, D_NOPE, D_ROPE, D_Q, D_V, LORA = (16, 128, 64, 192, 128, 64)
        SCALE = D_Q ** (-0.5)
        EPS = 1e-06

        def _rms_norm(x, weight, eps=EPS):
            xf = x.astype(jnp.float32)
            var = jnp.mean(xf * xf, axis=-1, keepdims=True)
            return (weight * (xf * jax.lax.rsqrt(var + eps))).astype(x.dtype)

        def _rotate_half(x):
            half = x.shape[-1] // 2
            return jnp.concatenate([-x[..., half:], x[..., :half]], axis=-1)
        key = jax.random.key(seed)
        ks = jax.random.split(key, 5)
        return {'hidden_states': jax.random.normal(ks[0], (B, S, HID), dtype=jnp.float32), 'Wq': jax.random.normal(ks[1], (NH * D_Q, HID), dtype=jnp.float32) * 0.02, 'Wkva': jax.random.normal(ks[2], (LORA + D_ROPE, HID), dtype=jnp.float32) * 0.02, 'kv_a_norm_weight': jnp.ones((LORA,), dtype=jnp.float32), 'Wkvb': jax.random.normal(ks[3], (NH * (D_NOPE + D_V), LORA), dtype=jnp.float32) * 0.02, 'Wo': jax.random.normal(ks[4], (HID, NH * D_V), dtype=jnp.float32) * 0.02, 'cos': jnp.ones((1, D_ROPE), dtype=jnp.float32), 'sin': jnp.zeros((1, D_ROPE), dtype=jnp.float32)}
    _L0_attn_in = _L0_attn_setup()

    def _L0_ffn_setup():
        import jax, jax.numpy as jnp
        import numpy as np
        DIM_IN = 256
        DIM_HIDDEN = 1024
        key = jax.random.key(seed)
        k_x, k_g, k_u, k_d = jax.random.split(key, 4)
        s_in = 1.0 / np.sqrt(DIM_IN)
        s_hid = 1.0 / np.sqrt(DIM_HIDDEN)
        x = jax.random.normal(k_x, (4, 256, DIM_IN), dtype=jnp.float32)
        w_gate = jax.random.uniform(k_g, (DIM_HIDDEN, DIM_IN), jnp.float32, -s_in, s_in)
        w_up = jax.random.uniform(k_u, (DIM_HIDDEN, DIM_IN), jnp.float32, -s_in, s_in)
        w_down = jax.random.uniform(k_d, (DIM_IN, DIM_HIDDEN), jnp.float32, -s_hid, s_hid)
        return {'x': x, 'w_gate': w_gate, 'w_up': w_up, 'w_down': w_down}
    _L0_ffn_in = _L0_ffn_setup()
    _d = {'L0_attn_hidden_states': _L0_attn_in['hidden_states'], 'L0_attn_Wq': _L0_attn_in['Wq'], 'L0_attn_Wkva': _L0_attn_in['Wkva'], 'L0_attn_kv_a_norm_weight': _L0_attn_in['kv_a_norm_weight'], 'L0_attn_Wkvb': _L0_attn_in['Wkvb'], 'L0_attn_Wo': _L0_attn_in['Wo'], 'L0_attn_cos': _L0_attn_in['cos'], 'L0_attn_sin': _L0_attn_in['sin'], 'L0_ffn_w_gate': _L0_ffn_in['w_gate'], 'L0_ffn_w_up': _L0_ffn_in['w_up'], 'L0_ffn_w_down': _L0_ffn_in['w_down']}
    _x0 = _d['L0_attn_hidden_states']
    _d['L0_attn_hidden_states'] = jax.random.normal(jax.random.fold_in(jax.random.key(seed), 1), (8, 256, 256), dtype=_x0.dtype)
    del _x0
    return _d

def reference(L0_attn_hidden_states, L0_attn_Wq, L0_attn_Wkva, L0_attn_kv_a_norm_weight, L0_attn_Wkvb, L0_attn_Wo, L0_attn_cos, L0_attn_sin, L0_ffn_w_gate, L0_ffn_w_up, L0_ffn_w_down):

    def _L0_attn_ref(hidden_states, Wq, Wkva, kv_a_norm_weight, Wkvb, Wo, cos, sin):
        import jax, jax.numpy as jnp
        import numpy as np
        B, S, HID = (2, 256, 256)
        NH, D_NOPE, D_ROPE, D_Q, D_V, LORA = (16, 128, 64, 192, 128, 64)
        SCALE = D_Q ** (-0.5)
        EPS = 1e-06

        def _rms_norm(x, weight, eps=EPS):
            xf = x.astype(jnp.float32)
            var = jnp.mean(xf * xf, axis=-1, keepdims=True)
            return (weight * (xf * jax.lax.rsqrt(var + eps))).astype(x.dtype)

        def _rotate_half(x):
            half = x.shape[-1] // 2
            return jnp.concatenate([-x[..., half:], x[..., :half]], axis=-1)
        b, s, _ = hidden_states.shape
        q = (hidden_states @ Wq.T).reshape(b, s, NH, D_Q).transpose(0, 2, 1, 3)
        q_nope, q_pe = (q[..., :D_NOPE], q[..., D_NOPE:])
        ckv = hidden_states @ Wkva.T
        compressed_kv, k_pe = (ckv[..., :LORA], ckv[..., LORA:])
        k_pe = k_pe.reshape(b, s, 1, D_ROPE).transpose(0, 2, 1, 3)
        kv = _rms_norm(compressed_kv, kv_a_norm_weight) @ Wkvb.T
        kv = kv.reshape(b, s, NH, D_NOPE + D_V).transpose(0, 2, 1, 3)
        k_nope, v = (kv[..., :D_NOPE], kv[..., D_NOPE:])
        q_pe = q_pe * cos + _rotate_half(q_pe) * sin
        k_pe = k_pe * cos + _rotate_half(k_pe) * sin
        q_full = jnp.concatenate([q_nope, q_pe], axis=-1)
        k_full = jnp.concatenate([k_nope, jnp.broadcast_to(k_pe, (b, NH, s, D_ROPE))], axis=-1)
        scores = jnp.einsum('bhqd,bhkd->bhqk', q_full, k_full) * SCALE
        causal = jnp.tril(jnp.ones((s, s), dtype=bool))
        scores = jnp.where(causal, scores, jnp.finfo(scores.dtype).min)
        attn = jax.nn.softmax(scores.astype(jnp.float32), axis=-1).astype(v.dtype)
        out = jnp.einsum('bhqk,bhkd->bhqd', attn, v)
        out = out.transpose(0, 2, 1, 3).reshape(b, s, NH * D_V)
        return out @ Wo.T

    def _L0_ffn_ref(x, w_gate, w_up, w_down):
        import jax, jax.numpy as jnp
        import numpy as np
        DIM_IN = 256
        DIM_HIDDEN = 1024
        gate = jnp.einsum('bsd,hd->bsh', x, w_gate)
        up = jnp.einsum('bsd,hd->bsh', x, w_up)
        gated = jax.nn.silu(gate) * up
        return jnp.einsum('bsh,dh->bsd', gated, w_down)
    x = L0_attn_hidden_states
    x = _layernorm(x + _L0_attn_ref(x, L0_attn_Wq, L0_attn_Wkva, L0_attn_kv_a_norm_weight, L0_attn_Wkvb, L0_attn_Wo, L0_attn_cos, L0_attn_sin), axis=-1)
    x = _layernorm(x + _L0_ffn_ref(x, L0_ffn_w_gate, L0_ffn_w_up, L0_ffn_w_down), axis=-1)
    return x

_drawn_inputs = setup_inputs


def setup_inputs(seed=0):
    import zlib

    import numpy as np

    out = dict(_drawn_inputs(seed))
    spreads = {'L0_attn_kv_a_norm_weight': (1.0, 0.6),
     'L0_attn_cos': (1.0, 0.6),
     'L0_attn_sin': (0.0, 0.8)}
    factors = {'L0_attn_Wq': 8.0}
    for name, (base, spread) in spreads.items():
        noise = np.random.default_rng([zlib.crc32(name.encode()), seed]).standard_normal(out[name].shape)
        drawn = base * np.exp(spread * noise) if base else spread * noise
        out[name] = jnp.asarray(drawn.astype(out[name].dtype))
    for name, factor in factors.items():
        out[name] = (out[name] * factor).astype(out[name].dtype)
    return out
```

```python
from contextlib import ExitStack

import concourse.bass as bass
from concourse import mybir
from concourse.alu_op_type import AluOpType as ALU

F32 = mybir.dt.float32
F32R = mybir.dt.float32r
ACT = mybir.ActivationFunctionType

P = 128
NB, S, HID = 8, 256, 256
NH, NOPE, ROPE, DV, LORA = 16, 128, 64, 128, 64
DQ = NOPE + ROPE
FF = 1024
NT = S // P
NC = HID // P
NP = NH // 2
NJ = FF // P
SCALE = float(DQ) ** -0.5
RMS_EPS = 1e-6
LN_EPS = 1e-5
MASKED = -3.0e38
TOP = 3.4e38
SLOTS = 6
SLOT = 896

READERS = {"WKVA": ("dve",), "XT": ("act",), "CKV": ("act",), "A": ("act", "dve"), "KT": ("act", "dve"),
           "WOT": ("act",), "B": ("act", "dve"), "F": ("act", "dve"), "OUT": ("dve",), "X1T": ("act", "dve"),
           "GU": ("act", "dve"), "DN": ("dve",)}

PROLOGUE = [("XT", 0, "Y"), ("WKVA", 0, "G"), ("A", 0, "Y"), ("CKV", 0, "G"), ("A", 1, "Y"), ("KT", 0, "G"),
            ("A", 2, "Y")]
FIRST = [
    [("A", 3, "Y"), ("WOT", 0, "G")],
    [("B", 0, "G"), ("A", 4, "Y"), ("WOT", 1, "G")],
    [("B", 1, "G"), ("A", 5, "Y"), ("XT", 1, "G"), ("WOT", 2, "Y")],
    [("B", 2, "G"), ("A", 6, "Y"), ("CKV", 1, "G"), ("F", 0, "Y"), ("WOT", 3, "G")],
    [("CNORM", 1, None), ("B", 3, "Y"), ("A", 7, "G"), ("F", 1, "Y"), ("WOT", 4, "G")],
    [("XSPLIT", 1, None), ("B", 4, "Y"), ("F", 2, "G"), ("F", 3, "Y"), ("F", 4, "G"), ("WOT", 5, "Y")],
    [("KT", 1, "G"), ("B", 5, "Y"), ("F", 5, "G"), ("F", 6, "Y"), ("F", 7, "G"), ("WOT", 6, "Y")],
    [("B", 6, "G"), ("F", 8, "Y"), ("WOT", 7, "G"), ("F", 9, "Y"), ("F", 10, "G"), ("F", 11, "Y"), ("B", 7, "G")],
]
MIDDLE = [
    [("OUTA", 0, None)],
    [("OUTB", 0, None), ("OUT", 0, "G"), ("OUT", 1, "Y"), ("LN1SUM", 0, None)],
    [("XT", 1, "Y"), ("X1T", 0, "G"), ("CKV", 1, "Y"), ("GU", 0, "G")],
    [("CNORM", 1, None), ("GU", 1, "Y"), ("GU", 2, "G")],
    [("GU", 3, "Y"), ("GU", 4, "G")],
    [("XSPLIT", 1, None), ("GU", 5, "Y"), ("GU", 6, "G")],
    [("KT", 1, "Y"), ("GU", 7, "G"), ("DNA", 0, None)],
    [("DN", 0, "Y"), ("DN", 1, "G"), ("LN2SUM", 0, None)],
]
OF_NEXT = ("XT", "CKV", "CNORM", "XSPLIT", "KT")
LAST = [[e for e in step if e[0] not in OF_NEXT] for step in MIDDLE]
EARLY = ("GU", "DN")
EPILOGUE = [("OUTA", 0, None), ("OUTB", 0, None), ("OUT", 0, "S"), ("OUT", 1, "R"), ("LN1SUM", 0, None),
            ("X1T", 0, "G"), ("GU", 0, "Y"), ("GU", 1, "S"), ("GU", 2, "R"), ("GU", 3, "G"), ("GU", 4, "Y"),
            ("GU", 5, "S"), ("GU", 6, "R"), ("GU", 7, "G"), ("DNA", 0, None), ("DNA", 1, None), ("DN", 0, "Y"),
            ("DN", 1, "S"), ("LN2SUM", 0, None)]
AHEAD = {"middle": (4, 0), "last": (4, 0), "epilogue": (NJ - 1, NJ - 1)}
DEFERRED = ("A", "WOT", "B", "F", "GU", "LN2SUM")
LOADS = [e[:2] for e in PROLOGUE + [e for step in FIRST for e in step] if e[0] in "ABF"]


def layer(nc, x, wq, wkva, norm_w, wkvb, wo, cos, sin, w_gate, w_up, w_down, out):
    with ExitStack() as ctx:
        def sb(name, shape, dt=F32):
            return ctx.enter_context(nc.sbuf_tensor(name, shape, dt))

        def pb(name, shape):
            return ctx.enter_context(nc.psum_tensor(name, shape, F32))

        def sem(name):
            return ctx.enter_context(nc.semaphore(name))

        ident = sb("ident", [P, P])
        mask = sb("mask", [P, 2 * P])
        cosb = sb("cosb", [P, 2, ROPE])
        sinb = sb("sinb", [P, 2, ROPE])
        rot = sb("rot", [P, 2, ROPE])
        ropet = sb("ropet", [P, 2, ROPE])
        kfold = sb("kfold", [P, 2, ROPE])
        normw = sb("normw", [P, LORA])
        mhalf = sb("mhalf", [P, 2])
        stage = sb("stage", [P, SLOTS, SLOT])
        wkva_raw = sb("wkva_raw", [P, HID])
        wkvat = sb("wkvat", [P, NC, P])
        a_hi = sb("a_hi", [P, NC, NH, P], F32R)
        a_lo = sb("a_lo", [P, NC, NH, P], F32R)
        wot = sb("wot", [P, 2, HID])
        b_hi = sb("b_hi", [P, NP, HID], F32R)
        b_lo = sb("b_lo", [P, NP, HID], F32R)
        ff_hi = [sb(f"{n}_hi", [P, NC, FF], F32R) for n in ("gate", "up")] + [sb("down_hi", [P, NJ, HID], F32R)]
        ff_lo = [sb(f"{n}_lo", [P, NC, FF], F32R) for n in ("gate", "up")] + [sb("down_lo", [P, NJ, HID], F32R)]
        x_in = sb("x_in", [P, NT, HID])
        x_res = sb("x_res", [P, NT, HID])
        xt = sb("xt", [P, NC, S])
        xt_hi = sb("xt_hi", [P, NC, S], F32R)
        xt_lo = sb("xt_lo", [P, NC, S], F32R)
        ckv = sb("ckv", [P, NT, P])
        squares = sb("squares", [P, NT, LORA])
        ssq = sb("ssq", [P, NT])
        msq = sb("msq", [P, NT])
        rms = sb("rms", [P, NT])
        kt = sb("kt", [P, P])
        kt_hi = sb("kt_hi", [P, S], F32R)
        kt_lo = sb("kt_lo", [P, S], F32R)
        c_parts = sb("c_parts", [P, NT, 2, LORA], F32R)
        q0 = sb("q0", [P, 2, 2, P])
        q1_hi = sb("q1_hi", [P, 2, 2, P], F32R)
        q1_lo = sb("q1_lo", [P, 2, 2, P], F32R)
        prob = sb("prob", [P, 2, 3 * P])
        nmax = sb("nmax", [P, 2, 2])
        rowsum = sb("rowsum", [P, 2, 2])
        rrow = sb("rrow", [P, 2, 2])
        pt_hi = sb("pt_hi", [P, 2, 3 * P], F32R)
        pt_lo = sb("pt_lo", [P, 2, 3 * P], F32R)
        o_low = sb("o_low", [LORA, 2, S])
        o_sum = sb("o_sum", [P, S])
        ot_hi = sb("ot_hi", [P, NP, S], F32R)
        ot_lo = sb("ot_lo", [P, NP, S], F32R)
        res = sb("res", [P, NT, HID])
        stats = sb("stats", [P, NT, 6])
        moments = sb("moments", [P, NT, 2])
        vareps = sb("vareps", [P, NT])
        rstd = sb("rstd", [P, NT])
        x1 = sb("x1", [P, NT, HID])
        x1t_hi = sb("x1t_hi", [P, NC, S], F32R)
        x1t_lo = sb("x1t_lo", [P, NC, S], F32R)
        act_g = sb("act_g", [P, 2, S])
        h_sum = sb("h_sum", [P, 2, S])
        h_hi = sb("h_hi", [P, NJ, S], F32R)
        h_lo = sb("h_lo", [P, NJ, S], F32R)
        y = sb("y", [P, NT, HID])

        q_ps = pb("q_ps", [P, 2, S])
        s_ps = [pb(f"s_ps{h}", [P, 512]) for h in range(2)]
        t_ps = [pb(f"t_ps{h}", [P, 512]) for h in range(2)]
        o_ps = pb("o_ps", [P, 2, S])
        bank = {"G": pb("g_ps", [P, 512]), "Y": pb("y_ps", [P, 512]), "S": s_ps[0], "R": s_ps[1]}

        x_in_loaded, x_res_loaded, small_loaded = sem("x_in_loaded"), sem("x_res_loaded"), sem("small_loaded")
        wkva_loaded = sem("wkva_loaded")
        slot_loaded = [sem(f"slot_loaded{i}") for i in range(SLOTS)]
        zeroed, ident_ready, mask_ready, rot_ready = (
            sem("zeroed"), sem("ident_ready"), sem("mask_ready"), sem("rot_ready"))
        rope_chain, rope_ready = sem("rope_chain"), sem("rope_ready")
        full = {k: sem(f"{k}_full") for k in bank}
        read = {(k, e): sem(f"{k}_read_by_{e}") for k in bank for e in ("act", "dve")}
        q_done, q_act_ready, q_lo_ready = sem("q_done"), sem("q_act_ready"), sem("q_lo_ready")
        s_done, max_ready, exp_ready, rrow_ready, prob_ready, t_done, pt_hi_ready, pt_lo_ready = (
            [sem(f"{n}{h}") for h in range(2)] for n in (
                "s_done", "max_ready", "exp_ready", "rrow_ready", "prob_ready", "t_done", "pt_hi_ready",
                "pt_lo_ready"))
        o_done, o_low_ready, o_sum_ready, ot_hi_ready, ot_ready = (
            sem("o_done"), sem("o_low_ready"), sem("o_sum_ready"), sem("ot_hi_ready"), sem("ot_ready"))
        ckv_copied, ssq_ready, msq_ready, rms_ready, c_ready = (
            sem("ckv_copied"), sem("ssq_ready"), sem("msq_ready"), sem("rms_ready"), sem("c_ready"))
        c_hi_ready, c_parts_ready, xt_hi_ready, xt_lo_ready = (
            sem("c_hi_ready"), sem("c_parts_ready"), sem("xt_hi_ready"), sem("xt_lo_ready"))
        out_half, x1_ready, y_ready, y_free = sem("out_half"), sem("x1_ready"), sem("y_ready"), sem("y_free")
        ln_chain, vareps_ready, rstd_ready = sem("ln_chain"), sem("vareps_ready"), sem("rstd_ready")
        dve_passed, pool_passed = sem("dve_passed"), sem("pool_passed")
        gated, h_hi_ready, h_ready = sem("gated"), sem("h_hi_ready"), sem("h_ready")

        def plan():
            now = {("full", k): 0 for k in bank} | {(k, e): 0 for k in bank for e in ("act", "dve")}
            last_use = dict.fromkeys(bank)
            uses = {}

            def add(part, events, slope):
                for kind, arg, k in events:
                    if k is None:
                        continue
                    before = [(e, now[k, e]) for e in ("act", "dve")
                              if last_use[k] and e in READERS[last_use[k]]]
                    now["full", k] += 1
                    for e in READERS[kind]:
                        now[k, e] += 1
                    last_use[k] = kind
                    uses[part, kind, arg] = (k, before, now["full", k], {e: now[k, e] for e in READERS[kind]},
                                             {i: slope(i) for i in now})

            flat = [e for step in MIDDLE for e in step]
            add("prologue", PROLOGUE, lambda i: 0)
            add("first", [e for step in FIRST for e in step], lambda i: 0)
            start = dict(now)
            add("middle", flat, lambda i: 0)
            growth = {i: now[i] - start[i] for i in now}
            for key, use in uses.items():
                if key[0] == "middle":
                    use[4].update(growth)
            for i in now:
                now[i] = start[i] + growth[i] * (NB - 2)
            add("last", [e for step in LAST for e in step], lambda i: 0)
            add("epilogue", EPILOGUE, lambda i: 0)
            return uses

        uses = plan()

        class Use:

            def __init__(self, part, kind, arg, b):
                self.bank, self.before, self.filled, self.after, self.growth = uses[part, kind, arg]
                self.b = b
                self.ps = bank[self.bank]

            def value(self, count, i):
                grow = self.growth[i]
                return self.b * grow + (count - grow) if grow else count

            def wait_free(self, pe):
                for e, count in self.before:
                    pe.wait_ge(read[self.bank, e], self.value(count, (self.bank, e)))

            def wait_full(self, eng):
                eng.wait_ge(full[self.bank], self.value(self.filled, ("full", self.bank)))

            def wait_read(self, eng, e):
                eng.wait_ge(read[self.bank, e], self.value(self.after[e], (self.bank, e)))

            @property
            def is_full(self):
                return full[self.bank]

            def read_by(self, e):
                return read[self.bank, e]

        def done(b, s, more=0):
            return b * NP + (s + 1 + more)

        def hold(eng, semaphore, count, passed):
            eng.wait_ge(semaphore, count)
            eng.sem_inc(passed, 1)

        def after(b, s, n):
            return (b, s + n) if s + n < NP else (b + 1, s + n - NP)

        def run(eng, prologue, step, epilogue):
            def steps(of, left=None):
                for b, s, events, part in of:
                    here = [(kind, arg, part, b) for kind, arg, _ in events]
                    leave = here[-1] if here[-1][0] in DEFERRED and (part, s) != ("last", NP - 1) else None
                    step(b, s, here[:-1] if leave else here, leave, left, part)
                    left = leave
                assert left is None

            prologue()
            steps([(0, s, FIRST[s], "first") for s in range(NP)] + [(1, 0, MIDDLE[0], "middle")])
            with eng.Fori(1, NB - 1) as b:
                steps([(b, s, MIDDLE[s], "middle") for s in range(1, NP)] + [(b + 1, 0, MIDDLE[0], "middle")])
            steps([(NB - 1, s, LAST[s], "last") for s in range(1, NP)])
            epilogue([(kind, arg, "epilogue", NB) for kind, arg, _ in EPILOGUE])

        def everything(events, leave):
            return events + [leave] * bool(leave)

        def follows(b, s, n):
            return not (isinstance(b, int) and b * NP + s + n >= NB * NP)

        a_of = {n: i for i, n in enumerate(LOADS)}

        def slot_of(kind, arg):
            return stage[:, a_of[kind, arg] % SLOTS, :], slot_loaded[a_of[kind, arg] % SLOTS]

        N_DMAS = {"A": 4, "B": 2, "F": 1}

        def slot_count(kind, arg):
            n = a_of[kind, arg]
            return 16 * sum(N_DMAS[k] for k, _ in LOADS[n % SLOTS:n + 1:SLOTS])

        block = ctx.enter_context(nc.Block())

        @block.sync
        def _(sp):
            def load_x(b):
                sp.dma_start(x_in[:, :, :], x[b].rearrange("(t p) c -> p t c", p=P)).then_inc(x_in_loaded, 16)

            def load_res(b):
                sp.dma_start(x_res[:, :, :], x[b].rearrange("(t p) c -> p t c", p=P)).then_inc(x_res_loaded, 16)

            def store_y(b):
                sp.wait_ge(y_ready, b + 1)
                sp.dma_start(out[b].rearrange("(t p) c -> p t c", p=P), y[:, :, :]).then_inc(y_free, 16)

            def load_weights(n):
                kind, i = LOADS[n]
                to, loaded = slot_of(kind, i)
                if n >= SLOTS:
                    k, j = LOADS[n - SLOTS]
                    part = "prologue" if ("prologue", k, j) in uses else "first"
                    Use(part, k, j, 0).wait_full(sp)
                if kind == "A":
                    heads = wq.rearrange("(h r) c -> r h c", r=DQ)[:, 2 * i:2 * i + 2, :]
                    kv = wkvb.rearrange("(h r) c -> r h c", r=NOPE + DV)[0:NOPE, 2 * i:2 * i + 2, :]
                    sp.dma_start(to[:, 0:512].rearrange("p (h c) -> p h c", h=2), heads[0:NOPE]).then_inc(loaded, 16)
                    sp.dma_start(to[:, 512:640].rearrange("p (h c) -> p h c", h=2), kv).then_inc(loaded, 16)
                    for h in range(2):
                        sp.dma_start(to[h * ROPE:(h + 1) * ROPE, 640:896], heads[NOPE:DQ, h, :]).then_inc(loaded, 16)
                elif kind == "B":
                    kv = wkvb.rearrange("(h r) c -> r h c", r=NOPE + DV)[NOPE:NOPE + DV, 2 * i:2 * i + 2, :]
                    cols = wo[:, 2 * i * DV:2 * (i + 1) * DV].rearrange("(o p) c -> p o c", p=P)
                    sp.dma_start(to[:, 0:512].rearrange("p (o c) -> p o c", o=2), cols).then_inc(loaded, 16)
                    sp.dma_start(to[:, 512:640].rearrange("p (h c) -> p h c", h=2), kv).then_inc(loaded, 16)
                else:
                    which, jj = divmod(i, 4)
                    if which < 2:
                        w = (w_gate, w_up)[which].rearrange("(j p) c -> p j c", p=P)[:, 2 * jj:2 * jj + 2, :]
                    else:
                        w = w_down[:, 2 * jj * P:2 * (jj + 1) * P].rearrange("(o p) c -> p o c", p=P)
                    sp.dma_start(to[:, 0:512].rearrange("p (j c) -> p j c", j=2), w).then_inc(loaded, 16)

            for n in range(len(LOADS)):
                load_weights(n)
                if n == 1:
                    Use("prologue", "XT", 0, 0).wait_full(sp)
                    load_x(1)
                if n == 5:
                    load_res(0)
            Use("first", "XT", 1, 0).wait_full(sp)
            load_x(2)
            with sp.Fori(1, NB - 2) as b:
                Use("middle", "OUT", 1, b).wait_read(sp, "dve")
                load_res(b)
                Use("middle", "XT", 1, b).wait_full(sp)
                load_x(b + 2)
                store_y(b - 1)
            Use("middle", "OUT", 1, NB - 2).wait_read(sp, "dve")
            load_res(NB - 2)
            store_y(NB - 3)
            Use("last", "OUT", 1, NB - 1).wait_read(sp, "dve")
            load_res(NB - 1)
            store_y(NB - 2)
            store_y(NB - 1)
            sp.wait_ge(y_free, 16 * (NB + 1))

        @block.tensor
        def _(pe):
            def three(ps, w_hi, w_lo, m_hi, m_lo, start, stop):
                nc.tensor.matmul(ps, w_hi, m_hi, start=start, stop=False)
                nc.tensor.matmul(ps, w_hi, m_lo, start=False, stop=False)
                return nc.tensor.matmul(ps, w_lo, m_hi, start=False, stop=stop)

            def transposes(b, s):
                for h in range(2):
                    pe.wait_ge(prob_ready[h], done(b, s))
                    for i in range(3):
                        last = nc.tensor.transpose(t_ps[h][:, i * P:(i + 1) * P], prob[:, h, i * P:(i + 1) * P],
                                                   ident[:, :])
                    last.then_inc(t_done[h], 1)

            def queries(b, s):
                if s == 0:
                    pe.wait_ge(xt_hi_ready, b + 1)
                    pe.wait_ge(xt_lo_ready, b + 1)
                if isinstance(b, int) and b == 0:
                    part = "prologue" if s < 3 else "first"
                    Use(part, "A", s, 0).wait_read(pe, "dve")
                for h in range(2):
                    n = 2 * s + h
                    for c in range(NC):
                        last = three(q_ps[:, h, :], a_hi[:, c, n, :], a_lo[:, c, n, :], xt_hi[:, c, :],
                                     xt_lo[:, c, :], c == 0, c == NC - 1)
                last.then_inc(q_done, 1)

            def scores(b, s):
                pe.wait_ge(q_lo_ready, done(b, s))
                i = s % 2
                for h in range(2):
                    nc.tensor.matmul(s_ps[h][:, 0:P], q0[:, i, h, :], kt[:, :], start=True, stop=True)
                    three(s_ps[h][:, P:3 * P], q1_hi[:, i, h, :], q1_lo[:, i, h, :], kt_hi[:, :], kt_lo[:, :],
                          True, True).then_inc(s_done[h], 1)

            def values(b, s):
                for h in range(2):
                    pe.wait_ge(pt_lo_ready[h], done(b, s))
                if s == 0:
                    pe.wait_ge(c_parts_ready, b + 1)
                if not (isinstance(b, int) and b == 0 and s == 0):
                    pe.wait_ge(o_sum_ready, done(b, s, -1))
                for k in range(NT):
                    cols = slice(0, S) if k == 0 else slice(S, S + P)
                    for pt in (pt_hi, pt_lo):
                        last = nc.tensor.matmul(o_ps[:, :, k * P:S], c_parts[:, k, :, :], pt[:, :, cols],
                                                start=(k == 0 and pt is pt_hi), stop=(k == 1 and pt is pt_lo))
                last.then_inc(o_done, 1)

            def project(b, part, pairs):
                for t in range(NT):
                    use = Use(part, "OUT", t, b)
                    for p in pairs:
                        if t == 0 and p == NP - 1:
                            pe.wait_ge(ot_ready, done(b - 1, NP - 1))
                        cols = slice(t * P, (t + 1) * P)
                        last = three(use.ps[:, 0:HID], ot_hi[:, p, cols], ot_lo[:, p, cols], b_hi[:, p, :],
                                     b_lo[:, p, :], p == 0, p == NP - 1)
                    if pairs[-1] == NP - 1:
                        last.then_inc(use.is_full, 1)
                    elif t == 1:
                        last.then_inc(out_half, 1)

            def down(ps, t, chunks):
                cols = slice(t * P, (t + 1) * P)
                for j in chunks:
                    last = three(ps[:, 0:HID], h_hi[:, j, cols], h_lo[:, j, cols], ff_hi[2][:, j, :],
                                 ff_lo[2][:, j, :], j == 0, j == NJ - 1)
                return last

            def event(kind, arg, part, b):
                if kind in ("CNORM", "XSPLIT", "LN1SUM", "LN2SUM", "OUT"):
                    return
                if kind == "OUTA":
                    for t in range(2):
                        Use(part, "OUT", t, b).wait_free(pe)
                    pe.wait_ge(ot_ready, done(b - 1, NP // 2 - 1))
                    project(b, part, range(0, NP // 2))
                    return
                if kind == "OUTB":
                    project(b, part, range(NP // 2, NP))
                    return
                if kind == "DNA":
                    use = Use(part, "DN", arg, b)
                    use.wait_free(pe)
                    pe.wait_ge(h_ready, (b - 1) * NJ + AHEAD[part][arg])
                    down(use.ps, arg, range(AHEAD[part][arg]))
                    return
                use = Use(part, kind, arg, b)
                ps = use.ps
                if kind != "DN" or AHEAD[part][arg] == 0:
                    use.wait_free(pe)
                if kind == "XT":
                    nb = b + arg
                    pe.wait_ge(x_in_loaded, (nb + 1) * 16)
                    if part == "prologue":
                        pe.wait_ge(ident_ready, 1)
                    for c in range(NC):
                        for t in range(NT):
                            last = nc.tensor.transpose(ps[:, c * S + t * P:c * S + (t + 1) * P],
                                                       x_in[:, t, c * P:(c + 1) * P], ident[:, :])
                elif kind == "WKVA":
                    pe.wait_ge(wkva_loaded, 16)
                    pe.wait_ge(rope_ready, 2)
                    for c in range(NC):
                        last = nc.tensor.matmul(ps[:, c * P:(c + 1) * P], wkva_raw[:, c * P:(c + 1) * P],
                                                kfold[:, :, :], start=True, stop=True)
                elif kind == "CKV":
                    if part == "prologue":
                        Use(part, "WKVA", 0, 0).wait_read(pe, "dve")
                    for t in range(NT):
                        for c in range(NC):
                            last = nc.tensor.matmul(ps[:, t * P:(t + 1) * P], xt[:, c, t * P:(t + 1) * P],
                                                    wkvat[:, c, :], start=(c == 0), stop=(c == NC - 1))
                elif kind == "KT":
                    pe.wait_ge(c_ready, b + arg + 1)
                    for t in range(NT):
                        last = nc.tensor.transpose(ps[:, t * P:(t + 1) * P], ckv[:, t, :], ident[:, :])
                elif kind == "A":
                    w, loaded = slot_of("A", arg)
                    pe.wait_ge(loaded, slot_count("A", arg))
                    for c in range(NC):
                        for h in range(2):
                            nc.tensor.matmul(ps[:, c * S + h * LORA:c * S + h * LORA + P],
                                             w[:, h * HID + c * P:h * HID + (c + 1) * P],
                                             w[:, 512 + h * LORA:512 + h * LORA + P], start=True, stop=True)
                        last = nc.tensor.matmul(ps[:, c * S + P:(c + 1) * S], w[:, 640 + c * P:640 + (c + 1) * P],
                                                ropet[:, :, :], start=True, stop=True)
                elif kind == "WOT":
                    w, loaded = slot_of("B", arg)
                    pe.wait_ge(loaded, slot_count("B", arg))
                    for h in range(2):
                        for o in range(NC):
                            last = nc.tensor.transpose(ps[:, h * HID + o * P:h * HID + (o + 1) * P],
                                                       w[:, o * 256 + h * P:o * 256 + (h + 1) * P], ident[:, :])
                elif kind == "B":
                    w, _ = slot_of("B", arg)
                    for h in range(2):
                        last = nc.tensor.matmul(ps[:, h * HID:(h + 1) * HID], w[:, 512:640], wot[:, h, :],
                                                start=True, stop=True)
                elif kind == "F":
                    w, loaded = slot_of("F", arg)
                    pe.wait_ge(loaded, slot_count("F", arg))
                    for j in range(2):
                        for c in range(2):
                            at = c * 256 + j * P if arg < 8 else j * 256 + c * P
                            src = j * 256 + c * P if arg < 8 else c * 256 + j * P
                            last = nc.tensor.transpose(ps[:, at:at + P], w[:, src:src + P], ident[:, :])
                elif kind == "X1T":
                    pe.wait_ge(x1_ready, b)
                    for c in range(NC):
                        for t in range(NT):
                            last = nc.tensor.transpose(ps[:, c * S + t * P:c * S + (t + 1) * P],
                                                       x1[:, t, c * P:(c + 1) * P], ident[:, :])
                elif kind == "GU":
                    if arg == 0:
                        Use(part, "X1T", 0, b).wait_read(pe, "dve")
                    cols = slice(arg * P, (arg + 1) * P)
                    for g in range(2):
                        for c in range(NC):
                            last = three(ps[:, g * S:(g + 1) * S], ff_hi[g][:, c, cols], ff_lo[g][:, c, cols],
                                         x1t_hi[:, c, :], x1t_lo[:, c, :], c == 0, c == NC - 1)
                elif kind == "DN":
                    pe.wait_ge(h_ready, b * NJ)
                    last = down(ps, arg, range(AHEAD[part][arg], NJ))
                last.then_inc(use.is_full, 1)

            def prologue():
                for kind, arg in (("XT", 0), ("WKVA", 0), ("A", 0), ("CKV", 0), ("A", 1)):
                    event(kind, arg, "prologue", 0)
                queries(0, 0)
                event("KT", 0, "prologue", 0)
                event("A", 2, "prologue", 0)
                Use("prologue", "KT", 0, 0).wait_read(pe, "dve")
                scores(0, 0)
                queries(0, 1)

            def step(b, s, events, leave, left, part):
                transposes(b, s)
                if follows(b, s, 1):
                    if s == NP - 1:
                        Use(part, "KT", 1, b).wait_read(pe, "dve")
                    scores(*after(b, s, 1))
                if follows(b, s, 2):
                    queries(*after(b, s, 2))
                early = [] if follows(b, s, 2) else [e for e in everything(events, leave) if e[0] in EARLY]
                for e in early:
                    event(*e)
                values(b, s)
                for e in everything(events, leave):
                    if e not in early:
                        event(*e)

            def epilogue(events):
                for e in events:
                    event(*e)

            run(pe, prologue, step, epilogue)

        @block.scalar
        def _(act):
            def copy(to, of):
                return nc.scalar.activation(to, of, ACT.Copy)

            def pt_high(b, s, h):
                act.wait_ge(t_done[h], done(b, s))
                copy(pt_hi[:, h, :], t_ps[h][:, 0:3 * P]).then_inc(pt_hi_ready[h], 1)

            def q_parts(b, s):
                act.wait_ge(q_done, done(b, s))
                copy(q0[:, s % 2, :, :], q_ps[:, :, 0:P])
                copy(q1_hi[:, s % 2, :, :], q_ps[:, :, P:S]).then_inc(q_act_ready, 1)

            def exps(b, s, h):
                act.wait_ge(max_ready[h], done(b, s))
                for t, cols in ((0, slice(0, P)), (1, slice(P, 3 * P))):
                    last = nc.scalar.activation(prob[:, h, cols], prob[:, h, cols], ACT.Exp,
                                                bias=nmax[:, h, t:t + 1], scale=-1.0,
                                                accum_out=rowsum[:, h, t:t + 1])
                last.then_inc(exp_ready[h], 1)

            def o_low_half(b, s):
                act.wait_ge(o_done, done(b, s))
                copy(o_low[:, :, :], o_ps[LORA:P, :, :]).then_inc(o_low_ready, 1)

            def event(kind, arg, part, b):
                if kind == "XSPLIT":
                    if part != "prologue":
                        act.wait_ge(q_done, done(b, NP - 1))
                    copy(xt_hi[:, :, :], xt[:, :, :]).then_inc(xt_hi_ready, 1)
                    return
                if kind not in READERS or "act" not in READERS[kind]:
                    return
                use = Use(part, kind, arg, b)
                ps = use.ps
                use.wait_full(act)
                if kind == "XT":
                    last = copy(xt[:, :, :], ps[:, :])
                elif kind == "CKV":
                    copy(ckv[:, :, :], ps[:, 0:NT * P]).then_inc(use.read_by("act"), 1)
                    use.wait_read(act, "act")
                    for t in range(NT):
                        last = nc.scalar.activation(squares[:, t, :], ckv[:, t, 0:LORA], ACT.Square,
                                                    accum_out=ssq[:, t:t + 1])
                    last.then_inc(ssq_ready, 1)
                    return
                elif kind == "KT":
                    copy(kt[:, :], ps[:, 0:P])
                    last = copy(kt_hi[:, :], ps[:, 0:S])
                elif kind == "A":
                    for c in range(NC):
                        last = copy(a_hi[:, c, 2 * arg:2 * arg + 2, :].rearrange("p h (k d) -> p k h d", k=2),
                                    ps[:, c * S:(c + 1) * S].rearrange("p (k h d) -> p k h d", k=2, h=2))
                elif kind == "WOT":
                    last = copy(wot[:, :, :], ps[:, :])
                elif kind == "B":
                    for h in range(2):
                        rows = slice(h * LORA, (h + 1) * LORA)
                        last = copy(b_hi[rows, arg, :], ps[rows, h * HID:(h + 1) * HID])
                elif kind == "F":
                    which, jj = divmod(arg, 4)
                    if which < 2:
                        last = copy(ff_hi[which][:, :, jj * 256:(jj + 1) * 256],
                                    ps[:, :].rearrange("p (c j) -> p c j", c=2))
                    else:
                        last = copy(ff_hi[2][:, 2 * jj:2 * jj + 2, :], ps[:, :])
                elif kind == "X1T":
                    last = copy(x1t_hi[:, :, :], ps[:, :])
                elif kind == "GU":
                    if arg >= 2:
                        Use(part, "GU", arg - 2, b).wait_read(act, "dve")
                    last = nc.scalar.activation(act_g[:, arg % 2, :], ps[:, 0:S], ACT.Tanh, scale=0.5)
                last.then_inc(use.read_by("act"), 1)

            def prologue():
                act.dma_start(x_in[:, :, :], x[0].rearrange("(t p) c -> p t c", p=P)).then_inc(x_in_loaded, 16)
                for to, of in ((cosb, cos), (sinb, sin)):
                    for k in range(2):
                        act.dma_start(to[:, k, :], of.partition_broadcast(P)).then_inc(small_loaded, 16)
                act.dma_start(wkva_raw[:, :], wkva).then_inc(wkva_loaded, 16)
                act.dma_start(normw[:, :], norm_w.rearrange("(a n) -> a n", a=1).partition_broadcast(P))\
                   .then_inc(small_loaded, 16)
                event("XT", 0, "prologue", 0)
                Use("prologue", "XT", 0, 0).wait_read(act, "act")
                event("XSPLIT", 0, "prologue", 0)
                for kind, arg in (("A", 0), ("CKV", 0), ("A", 1)):
                    event(kind, arg, "prologue", 0)
                q_parts(0, 0)
                event("KT", 0, "prologue", 0)
                event("A", 2, "prologue", 0)
                for h in range(2):
                    exps(0, 0, h)
                q_parts(0, 1)

            def step(b, s, events, leave, left, part):
                for h in range(2):
                    pt_high(b, s, h)
                if follows(b, s, 1):
                    for h in range(2):
                        exps(*after(b, s, 1), h)
                if follows(b, s, 2):
                    q_parts(*after(b, s, 2))
                o_low_half(b, s)
                for e in everything(events, leave):
                    event(*e)

            def epilogue(events):
                for e in events:
                    event(*e)

            run(act, prologue, step, epilogue)

        @block.vector
        def _(dve):
            tt, stt = nc.vector.tensor_tensor, nc.vector.scalar_tensor_tensor

            def low(to, of, high):
                return tt(to, of, high.bitcast(F32), ALU.subtract)

            def pt_low(b, s, h):
                dve.wait_ge(pt_hi_ready[h], done(b, s))
                low(pt_lo[:, h, :], t_ps[h][:, 0:3 * P], pt_hi[:, h, :]).then_inc(pt_lo_ready[h], 1)

            def maxima(b, s, h):
                hold(dve, s_done[h], done(b, s), dve_passed)
                for t, cols in ((0, slice(0, P)), (1, slice(P, 3 * P))):
                    last = nc.vector.tensor_tensor_reduce(
                        out=prob[:, h, cols], in0=s_ps[h][:, cols], in1=mask[:, (1 - t) * P:2 * P], scale=-SCALE,
                        scalar=TOP, op0=ALU.add, op1=ALU.min, accum_out=nmax[:, h, t:t + 1])
                last.then_inc(max_ready[h], 1)

            def row_reciprocals(b, s, h):
                dve.wait_ge(exp_ready[h], done(b, s))
                nc.vector.reciprocal(rrow[:, h, :], rowsum[:, h, :]).then_inc(rrow_ready[h], 1)

            def q_low(b, s):
                dve.wait_ge(q_act_ready, done(b, s))
                low(q1_lo[:, s % 2, :, :], q_ps[:, :, P:S], q1_hi[:, s % 2, :, :]).then_inc(q_lo_ready, 1)

            def o_add(b, s):
                dve.wait_ge(o_low_ready, done(b, s))
                if not (isinstance(b, int) and b == 0 and s == 0):
                    dve.wait_ge(ot_ready, done(b, s, -1))
                for h in range(2):
                    last = tt(o_sum[h * LORA:(h + 1) * LORA, :], o_ps[0:LORA, h, :], o_low[:, h, :], ALU.add)
                last.then_inc(o_sum_ready, 1)

            def ln_sum(n, residual, banks):
                for t, use in enumerate(banks):
                    use.wait_full(dve)
                    tt(res[:, t, :], use.ps[:, 0:HID], residual[:, t, :], ALU.add).then_inc(use.read_by("dve"), 1)
                    use.wait_read(dve, "dve")
                    last = nc.vector.bn_stats(stats[:, t, :], res[:, t, :])
                last.then_inc(ln_chain, 1)
                hold(dve, ln_chain, n * 2 + 1, dve_passed)
                for t in range(NT):
                    last = nc.vector.bn_aggr(moments[:, t, :], stats[:, t, :])
                last.then_inc(ln_chain, 1)
                dve.wait_ge(ln_chain, n * 2 + 2)
                nc.vector.tensor_scalar(vareps[:, :], moments[:, :, 1], LN_EPS, None, ALU.add).then_inc(vareps_ready, 1)

            def ln_scale(n, to, ready):
                dve.wait_ge(rstd_ready, n + 1)
                for t in range(NT):
                    last = nc.vector.tensor_scalar(to[:, t, :], res[:, t, :], moments[:, t, 0:1], rstd[:, t:t + 1],
                                                   ALU.subtract, ALU.mult)
                last.then_inc(ready, 1)

            def ln2_scale(f):
                dve.wait_ge(y_free, f * 16 + 16)
                ln_scale(f * 2 + 1, y, y_ready)

            def event(kind, arg, part, b):
                if kind == "XSPLIT":
                    dve.wait_ge(xt_hi_ready, b + arg + 1)
                    low(xt_lo[:, :, :], xt[:, :, :], xt_hi[:, :, :]).then_inc(xt_lo_ready, 1)
                elif kind == "CNORM":
                    dve.wait_ge(rms_ready, b + arg + 1)
                    for t in range(NT):
                        last = stt(ckv[:, t, 0:LORA], ckv[:, t, 0:LORA], rms[:, t:t + 1], normw[:, :], ALU.mult,
                                   ALU.mult)
                    last.then_inc(c_ready, 1)
                elif kind == "CKV":
                    dve.wait_ge(ssq_ready, b + arg + 1)
                    nc.vector.tensor_scalar(msq[:, :], ssq[:, :], 1.0 / LORA, RMS_EPS, ALU.mult, ALU.add)\
                      .then_inc(msq_ready, 1)
                elif kind == "LN1SUM":
                    dve.wait_ge(x_res_loaded, b * 16)
                    if part == "epilogue":
                        dve.wait_ge(y_ready, NB - 1)
                    ln_sum((b - 1) * 2, x_res, [Use(part, "OUT", t, b) for t in range(NT)])
                elif kind == "LN2SUM":
                    dve.wait_ge(x1_ready, b)
                    ln_sum((b - 1) * 2 + 1, x1, [Use(part, "DN", t, b) for t in range(NT)])
                if kind not in ("WKVA", "A", "KT", "B", "F", "X1T", "GU"):
                    return
                use = Use(part, kind, arg, b)
                ps = use.ps
                if kind == "WKVA":
                    use.wait_full(dve)
                    last = nc.vector.tensor_copy(wkvat[:, :, :], ps[:, 0:NC * P])
                else:
                    use.wait_read(dve, "act")
                if kind == "KT":
                    last = low(kt_lo[:, :], ps[:, 0:S], kt_hi[:, :])
                elif kind == "A":
                    for c in range(NC):
                        last = low(a_lo[:, c, 2 * arg:2 * arg + 2, :].rearrange("p h (k d) -> p k h d", k=2),
                                   ps[:, c * S:(c + 1) * S].rearrange("p (k h d) -> p k h d", k=2, h=2),
                                   a_hi[:, c, 2 * arg:2 * arg + 2, :].rearrange("p h (k d) -> p k h d", k=2))
                elif kind == "B":
                    for h in range(2):
                        rows = slice(h * LORA, (h + 1) * LORA)
                        last = low(b_lo[rows, arg, :], ps[rows, h * HID:(h + 1) * HID], b_hi[rows, arg, :])
                elif kind == "F":
                    which, jj = divmod(arg, 4)
                    if which < 2:
                        cols = slice(jj * 256, (jj + 1) * 256)
                        last = low(ff_lo[which][:, :, cols], ps[:, :].rearrange("p (c j) -> p c j", c=2),
                                   ff_hi[which][:, :, cols])
                    else:
                        last = low(ff_lo[2][:, 2 * jj:2 * jj + 2, :], ps[:, :].rearrange("p (j c) -> p j c", j=2),
                                   ff_hi[2][:, 2 * jj:2 * jj + 2, :])
                elif kind == "X1T":
                    last = low(x1t_lo[:, :, :], ps[:, :].rearrange("p (c s) -> p c s", c=NC), x1t_hi[:, :, :])
                elif kind == "GU":
                    i = arg % 2
                    stt(act_g[:, i, :], act_g[:, i, :], 1.0, ps[:, 0:S], ALU.add, ALU.mult).then_inc(gated, 1)
                    dve.wait_ge(gated, (b - 1) * NJ + (arg + 1))
                    if arg >= 2:
                        dve.wait_ge(h_ready, (b - 1) * NJ + (arg - 1))
                    last = stt(h_sum[:, i, :], act_g[:, i, :], 0.5, ps[:, S:2 * S], ALU.mult, ALU.mult)
                last.then_inc(use.read_by("dve"), 1)

            def prologue():
                dve.wait_ge(small_loaded, 16 * 5)
                dve.wait_ge(ident_ready, 1)
                dve.wait_ge(rot_ready, 2)
                tt(rot[:, :, :], rot[:, :, :], sinb[:, :, :], ALU.mult).then_inc(rope_chain, 1)
                tt(cosb[:, :, :], cosb[:, :, :], ident[:, :].rearrange("p (k d) -> p k d", k=2), ALU.mult)\
                    .then_inc(rope_chain, 1)
                dve.wait_ge(rope_chain, 2)
                tt(ropet[:, :, :], rot[:, :, :], cosb[:, :, :], ALU.add).then_inc(rope_ready, 1)
                nc.vector.tensor_copy(kfold[:, 0, :], ident[:, 0:LORA])
                dve.wait_ge(rope_ready, 1)
                nc.vector.tensor_copy(kfold[:, 1, :], ropet[:, 1, :]).then_inc(rope_ready, 1)
                event("WKVA", 0, "prologue", 0)
                for kind, arg in (("XSPLIT", 0), ("A", 0), ("CKV", 0), ("CNORM", 0), ("A", 1)):
                    event(kind, arg, "prologue", 0)
                q_low(0, 0)
                event("KT", 0, "prologue", 0)
                event("A", 2, "prologue", 0)
                dve.wait_ge(mask_ready, 1)
                for h in range(2):
                    maxima(0, 0, h)
                for h in range(2):
                    row_reciprocals(0, 0, h)
                q_low(0, 1)

            def step(b, s, events, leave, left, part):
                for h in range(2):
                    pt_low(b, s, h)
                if follows(b, s, 1):
                    for h in range(2):
                        maxima(*after(b, s, 1), h)
                if left:
                    event(*left)
                if s == 2 and part != "first":
                    ln_scale((b - 1) * 2, x1, x1_ready)
                if follows(b, s, 1):
                    for h in range(2):
                        row_reciprocals(*after(b, s, 1), h)
                if follows(b, s, 2):
                    q_low(*after(b, s, 2))
                o_add(b, s)
                if left and left[0] == "LN2SUM":
                    ln2_scale(b - 2)
                for e in events:
                    event(*e)

            def epilogue(events):
                ln2_scale(NB - 2)
                for e in events:
                    event(*e)
                    if e[0] == "LN1SUM":
                        ln_scale((NB - 1) * 2, x1, x1_ready)
                ln2_scale(NB - 1)

            run(dve, prologue, step, epilogue)

        @block.gpsimd
        def _(pool):
            def keep(to, of):
                return nc.gpsimd.tensor_scalar(to, of, 1.0, 1.0, ALU.mult, ALU.mult)

            def normalise(b, s, h):
                hold(pool, rrow_ready[h], done(b, s), pool_passed)
                for t, cols in ((0, slice(0, P)), (1, slice(P, 3 * P))):
                    last = nc.gpsimd.tensor_scalar(prob[:, h, cols], prob[:, h, cols], rrow[:, h, t:t + 1], 1.0,
                                                   ALU.mult, ALU.mult)
                last.then_inc(prob_ready[h], 1)

            def o_split(b, s):
                pool.wait_ge(o_sum_ready, done(b, s))
                if not (isinstance(b, int) and b == 0):
                    if s == 0:
                        pool.wait_ge(out_half, b)
                    if s == NP // 2:
                        Use("middle", "OUT", 1, b).wait_full(pool)
                pool.sem_inc(pool_passed, 1)
                keep(ot_hi[:, s, :], o_sum[:, :]).then_inc(ot_hi_ready, 1)
                pool.wait_ge(ot_hi_ready, done(b, s))
                nc.gpsimd.tensor_tensor(ot_lo[:, s, :], o_sum[:, :], ot_hi[:, s, :].bitcast(F32), ALU.subtract)\
                    .then_inc(ot_ready, 1)

            def c_split(nb):
                pool.wait_ge(c_ready, nb + 1)
                if not isinstance(nb, int) or nb > 0:
                    pool.wait_ge(o_done, nb * NP)
                pool.sem_inc(pool_passed, 1)
                keep(c_parts[:, :, 0, :], ckv[:, :, 0:LORA]).then_inc(c_hi_ready, 1)
                pool.wait_ge(c_hi_ready, nb + 1)
                nc.gpsimd.tensor_tensor(c_parts[:, :, 1, :], ckv[:, :, 0:LORA], c_parts[:, :, 0, :].bitcast(F32),
                                        ALU.subtract).then_inc(c_parts_ready, 1)

            def event(kind, arg, part, b):
                if kind == "CKV":
                    pool.wait_ge(msq_ready, b + arg + 1)
                    nc.gpsimd.tensor_tensor(rms[:, :], msq[:, :], mhalf[:, :], ALU.pow).then_inc(rms_ready, 1)
                elif kind in ("LN1SUM", "LN2SUM"):
                    n = (b - 1) * 2 + (kind == "LN2SUM")
                    pool.wait_ge(vareps_ready, n + 1)
                    nc.gpsimd.tensor_tensor(rstd[:, :], vareps[:, :], mhalf[:, :], ALU.pow).then_inc(rstd_ready, 1)
                elif kind == "GU":
                    Use(part, kind, arg, b).wait_read(pool, "dve")
                    pool.sem_inc(pool_passed, 1)
                    keep(h_hi[:, arg, :], h_sum[:, arg % 2, :]).then_inc(h_hi_ready, 1)
                    pool.wait_ge(h_hi_ready, (b - 1) * NJ + (arg + 1))
                    nc.gpsimd.tensor_tensor(h_lo[:, arg, :], h_sum[:, arg % 2, :], h_hi[:, arg, :].bitcast(F32),
                                            ALU.subtract).then_inc(h_ready, 1)

            def prologue():
                nc.gpsimd.memset(ident[:, :], 0.0).then_inc(zeroed, 1)
                nc.gpsimd.memset(rot[:, :, :], 0.0).then_inc(zeroed, 1)
                nc.gpsimd.memset(mask[:, :], 0.0).then_inc(zeroed, 1)
                nc.gpsimd.memset(mhalf[:, :], -0.5)
                nc.gpsimd.memset(y[:, :, :], 0.0).then_inc(y_free, 16)
                pool.wait_ge(zeroed, 3)
                nc.gpsimd.affine_select(out=ident[:, :], in_=ident[:, :], compare_op=ALU.not_equal, fill=1.0, base=0,
                                        pattern=[[-1, P]], channel_multiplier=1).then_inc(ident_ready, 1)
                half = ROPE // 2
                for k, (sign, base) in enumerate(((-1.0, -half), (1.0, 0))):
                    v = rot[:, :, k * half:(k + 1) * half]
                    nc.gpsimd.affine_select(out=v, in_=v, compare_op=ALU.not_equal, fill=sign, base=base,
                                            pattern=[[-ROPE, 2], [-1, half]], channel_multiplier=1)\
                        .then_inc(rot_ready, 1)
                nc.gpsimd.affine_select(out=mask[:, P:2 * P], in_=mask[:, P:2 * P], compare_op=ALU.is_ge, fill=MASKED,
                                        base=0, pattern=[[-1, P]], channel_multiplier=1).then_inc(mask_ready, 1)
                event("CKV", 0, "prologue", 0)
                c_split(0)
                for h in range(2):
                    normalise(0, 0, h)

            def step(b, s, events, leave, left, part):
                if left and left[0] == "LN2SUM":
                    event(*left)
                if follows(b, s, 1):
                    for h in range(2):
                        normalise(*after(b, s, 1), h)
                if left and left[0] != "LN2SUM":
                    event(*left)
                if s == NP - 1 and follows(b, s, 1):
                    c_split(b + 1)
                o_split(b, s)
                for e in events:
                    event(*e)

            def epilogue(events):
                for e in events:
                    event(*e)

            run(pool, prologue, step, epilogue)


_INS = ["L0_attn_hidden_states", "L0_attn_Wq", "L0_attn_Wkva", "L0_attn_kv_a_norm_weight", "L0_attn_Wkvb",
        "L0_attn_Wo", "L0_attn_cos", "L0_attn_sin", "L0_ffn_w_gate", "L0_ffn_w_up", "L0_ffn_w_down"]


def kernel(**inputs):
    import numpy as _np
    import concourse.bacc as _bacc
    from concourse import mybir as _mybir
    from concourse.bass_utils import run_bass_kernel_spmd as _run

    nc = _bacc.Bacc("TRN2", target_bir_lowering=False, num_devices=1)
    arrays, args = {}, []
    for name in _INS:
        a = _np.ascontiguousarray(inputs[name])
        arrays[f"in_{name}_dram"] = a
        args.append(nc.dram_tensor(f"in_{name}_dram", a.shape, _mybir.dt.from_np(a.dtype), kind="ExternalInput").ap())
    out = nc.dram_tensor("out_dram", (NB, S, HID), _mybir.dt.float32, kind="ExternalOutput").ap()
    layer(nc, *args, out)
    return _run(nc, [arrays], core_ids=[0]).results[0]["out_dram"]
```

```python
from contextlib import ExitStack

import concourse.bass as bass
from concourse import mybir
from concourse.alu_op_type import AluOpType as ALU

F32 = mybir.dt.float32
F32R = mybir.dt.float32r
ACT = mybir.ActivationFunctionType

P = 128
NB, S, HID = 8, 256, 256
NH, NOPE, ROPE, DV, LORA = 16, 128, 64, 128, 64
DQ = NOPE + ROPE
FF = 1024
NT = S // P
NC = HID // P
NP = NH // 2
NJ = FF // P
SCALE = float(DQ) ** -0.5
RMS_EPS = 1e-6
LN_EPS = 1e-5
MASKED = -3.0e38
TOP = 3.4e38
SLOTS = 6
SLOT = 896

READERS = {"WKVA": ("dve",), "XT": ("act",), "CKV": ("act",), "A": ("act", "dve"), "KT": ("act", "dve"),
           "WOT": ("dve",), "B": ("act", "dve"), "F": ("act", "dve"), "OUT": ("dve",), "X1T": ("act", "dve"),
           "GU": ("act", "dve"), "DN": ("dve",)}

PROLOGUE = [("XT", 0, "Y"), ("WKVA", 0, "G"), ("CKV", 0, "Y"), ("A", 0, "G"), ("KT", 0, "S"), ("A", 1, "Y"),
            ("A", 2, "G"), ("F", 0, "Y"), ("F", 1, "G")]
FIRST = [
    ([("WOT", 0, "Y"), ("A", 3, "G")], [("B", 0, "Y"), ("F", 2, "G")]),
    ([("WOT", 1, "Y"), ("A", 4, "G")], [("B", 1, "Y"), ("F", 3, "G")]),
    ([("WOT", 2, "Y"), ("A", 5, "G")], [("B", 2, "Y"), ("XT", 1, "G")]),
    ([("WOT", 3, "Y"), ("A", 6, "G")], [("B", 3, "Y"), ("CKV", 1, "G")]),
    ([("WOT", 4, "Y"), ("A", 7, "G")], [("CNORM", 1, None), ("B", 4, "Y"), ("F", 4, "G")]),
    ([("XSPLIT", 1, None), ("WOT", 5, "Y"), ("F", 5, "G")], [("B", 5, "Y"), ("F", 6, "G")]),
    ([("WOT", 6, "Y"), ("KT", 1, "G")], [("B", 6, "Y"), ("F", 7, "G"), ("F", 8, "Y")]),
    ([("WOT", 7, "G"), ("F", 9, "Y")], [("B", 7, "G"), ("F", 10, "Y"), ("F", 11, "G")]),
]
MIDDLE = [
    ([("OUTA", 0, None)], [("OUT", 0, "G")]),
    ([("OUT", 1, "Y")], [("XT", 1, "G")]),
    ([("CKV", 1, "Y")], [("X1T", 0, "G")]),
    ([("GU", 0, "Y")], [("CNORM", 1, None), ("GU", 1, "G"), ("GU", 2, "Y")]),
    ([("GU", 3, "G")], [("GU", 4, "Y"), ("GU", 5, "G")]),
    ([("XSPLIT", 1, None), ("GU", 6, "Y"), ("GU", 7, "G")], []),
    ([("KT", 1, "Y")], [("DN", 0, "G")]),
    ([("DN", 1, "Y")], []),
]
OF_NEXT = ("XT", "CKV", "CNORM", "XSPLIT", "KT")


def in_last(s, ahead, behind):
    if s == NP - 2:
        ahead, behind = ahead + behind, []
    if s >= NP - 2:
        ahead = [(kind, arg, {"G": "Y", "Y": "G"}[k]) for kind, arg, k in ahead]
    return tuple([e for e in events if e[0] not in OF_NEXT] for events in (ahead, behind))


LAST = [in_last(s, *events) for s, events in enumerate(MIDDLE)]
EPILOGUE = [("OUTA", 0, None), ("OUT", 0, "S"), ("OUT", 1, "R"),
            ("X1T", 0, "G"), ("GU", 0, "Y"), ("GU", 1, "S"), ("GU", 2, "R"), ("GU", 3, "G"), ("GU", 4, "Y"),
            ("GU", 5, "S"), ("GU", 6, "R"), ("GU", 7, "G"), ("DNA", 0, None), ("DNA", 1, None), ("DN", 0, "Y"),
            ("DN", 1, "S")]
AHEAD = {"middle": 0, "last": 0, "epilogue": NJ - 1}


def in_order(steps):
    return [e for ahead, behind in steps for e in ahead + behind]


DEFERRED = ("A", "WOT", "B", "F", "GU", "OUT", "DN")
LOADS = [e[:2] for e in PROLOGUE + in_order(FIRST) if e[0] in "ABF"]


def layer(nc, x, wq, wkva, norm_w, wkvb, wo, cos, sin, w_gate, w_up, w_down, out):
    with ExitStack() as ctx:
        def sb(name, shape, dt=F32):
            return ctx.enter_context(nc.sbuf_tensor(name, shape, dt))

        def pb(name, shape):
            return ctx.enter_context(nc.psum_tensor(name, shape, F32))

        def sem(name):
            return ctx.enter_context(nc.semaphore(name))

        ident = sb("ident", [P, P])
        mask = sb("mask", [P, 2 * P])
        cosb = sb("cosb", [P, ROPE])
        sinb = sb("sinb", [P, ROPE])
        rot = sb("rot", [P, 2, ROPE])
        ropet = sb("ropet", [P, 2, ROPE])
        kfold = sb("kfold", [P, 2, ROPE])
        normw = sb("normw", [P, LORA])
        mhalf = sb("mhalf", [P, 2])
        stage = sb("stage", [P, SLOTS, SLOT])
        wkva_raw = sb("wkva_raw", [P, HID])
        wkvat = sb("wkvat", [P, NC, P])
        a_hi = sb("a_hi", [P, NC, NH, P], F32R)
        a_lo = sb("a_lo", [P, NC, NH, P], F32R)
        wot = sb("wot", [P, 2, HID])
        b_hi = sb("b_hi", [P, NP, HID], F32R)
        b_lo = sb("b_lo", [P, NP, HID], F32R)
        ff_hi = [sb(f"{n}_hi", [P, NC, FF], F32R) for n in ("gate", "up")] + [sb("down_hi", [P, NJ, HID], F32R)]
        ff_lo = [sb(f"{n}_lo", [P, NC, FF], F32R) for n in ("gate", "up")] + [sb("down_lo", [P, NJ, HID], F32R)]
        x_in = sb("x_in", [P, NT, HID])
        x_res = sb("x_res", [P, NT, HID])
        xt = sb("xt", [P, NC, S])
        xt_hi = sb("xt_hi", [P, NC, S], F32R)
        xt_lo = sb("xt_lo", [P, NC, S], F32R)
        ckv = sb("ckv", [P, NT, P])
        squares = sb("squares", [P, NT, LORA])
        ssq = sb("ssq", [P, NT])
        msq = sb("msq", [P, NT])
        rms = sb("rms", [P, NT])
        kt = sb("kt", [P, P])
        kt_hi = sb("kt_hi", [P, S], F32R)
        kt_lo = sb("kt_lo", [P, S], F32R)
        c_parts = sb("c_parts", [P, NT, 2, LORA], F32R)
        q0 = sb("q0", [P, 2, 2, P])
        q1_hi = sb("q1_hi", [P, 2, 2, P], F32R)
        q1_lo = sb("q1_lo", [P, 2, 2, P], F32R)
        prob = sb("prob", [P, 2, 3 * P])
        nmax = sb("nmax", [P, 2, 2])
        rowsum = sb("rowsum", [P, 2, 2])
        rrow = sb("rrow", [P, 2, 2])
        pt_hi = sb("pt_hi", [P, 2, 3 * P], F32R)
        pt_lo = sb("pt_lo", [P, 2, 3 * P], F32R)
        o_low = sb("o_low", [LORA, 2, S])
        o_sum = sb("o_sum", [P, S])
        ot_hi = sb("ot_hi", [P, NP, S], F32R)
        ot_lo = sb("ot_lo", [P, NP, S], F32R)
        res = sb("res", [P, NT, HID])
        stats = sb("stats", [P, NT, 6])
        moments = sb("moments", [P, NT, 2])
        vareps = sb("vareps", [P, NT])
        rstd = sb("rstd", [P, NT])
        x1 = sb("x1", [P, NT, HID])
        x1t_hi = sb("x1t_hi", [P, NC, S], F32R)
        x1t_lo = sb("x1t_lo", [P, NC, S], F32R)
        act_g = sb("act_g", [P, 2, S])
        h_sum = sb("h_sum", [P, 2, S])
        h_hi = sb("h_hi", [P, NJ, S], F32R)
        h_lo = sb("h_lo", [P, NJ, S], F32R)
        y = sb("y", [P, NT, HID])

        q_ps = pb("q_ps", [P, 2, S])
        s_ps = [pb(f"s_ps{h}", [P, 512]) for h in range(2)]
        t_ps = [pb(f"t_ps{h}", [P, 512]) for h in range(2)]
        o_ps = pb("o_ps", [P, 2, S])
        bank = {"G": pb("g_ps", [P, 512]), "Y": pb("y_ps", [P, 512]), "S": s_ps[0], "R": s_ps[1]}

        x_in_loaded, x_res_loaded, rope_loaded = sem("x_in_loaded"), sem("x_res_loaded"), sem("rope_loaded")
        wkva_loaded, normw_loaded = sem("wkva_loaded"), sem("normw_loaded")
        slot_loaded = [sem(f"slot_loaded{i}") for i in range(SLOTS)]
        zeroed, ident_ready, mask_ready, rot_ready = (
            sem("zeroed"), sem("ident_ready"), sem("mask_ready"), sem("rot_ready"))
        rope_chain, rope_ready = sem("rope_chain"), sem("rope_ready")
        full = {k: sem(f"{k}_full") for k in bank}
        read = {(k, e): sem(f"{k}_read_by_{e}") for k in bank for e in ("act", "dve")}
        q_done, q_act_ready, q_lo_ready = sem("q_done"), sem("q_act_ready"), sem("q_lo_ready")
        s_done, max_ready, exp_ready, rrow_ready, prob_ready, t_done, pt_hi_ready, pt_lo_ready = (
            [sem(f"{n}{h}") for h in range(2)] for n in (
                "s_done", "max_ready", "exp_ready", "rrow_ready", "prob_ready", "t_done", "pt_hi_ready",
                "pt_lo_ready"))
        o_done, o_low_ready, o_sum_ready, ot_hi_ready, ot_ready = (
            sem("o_done"), sem("o_low_ready"), sem("o_sum_ready"), sem("ot_hi_ready"), sem("ot_ready"))
        ckv_copied, ssq_ready, msq_ready, rms_ready, c_ready = (
            sem("ckv_copied"), sem("ssq_ready"), sem("msq_ready"), sem("rms_ready"), sem("c_ready"))
        c_hi_ready, c_parts_ready, xt_hi_ready, xt_lo_ready = (
            sem("c_hi_ready"), sem("c_parts_ready"), sem("xt_hi_ready"), sem("xt_lo_ready"))
        out_half, x1_ready, y_ready, y_free = sem("out_half"), sem("x1_ready"), sem("y_ready"), sem("y_free")
        ln_chain, vareps_ready, rstd_ready = sem("ln_chain"), sem("vareps_ready"), sem("rstd_ready")
        dve_passed, pool_passed = sem("dve_passed"), sem("pool_passed")
        gated, h_hi_ready, h_ready = sem("gated"), sem("h_hi_ready"), sem("h_ready")

        def plan():
            now = {("full", k): 0 for k in bank} | {(k, e): 0 for k in bank for e in ("act", "dve")}
            last_use = dict.fromkeys(bank)
            uses = {}

            def add(part, events, slope):
                for kind, arg, k in events:
                    if k is None:
                        continue
                    before = [(e, now[k, e]) for e in ("act", "dve")
                              if last_use[k] and e in READERS[last_use[k]]]
                    now["full", k] += 1
                    for e in READERS[kind]:
                        now[k, e] += 1
                    last_use[k] = kind
                    uses[part, kind, arg] = (k, before, now["full", k], {e: now[k, e] for e in READERS[kind]},
                                             {i: slope(i) for i in now})

            add("prologue", PROLOGUE, lambda i: 0)
            add("first", in_order(FIRST), lambda i: 0)
            start = dict(now)
            add("middle", in_order(MIDDLE), lambda i: 0)
            growth = {i: now[i] - start[i] for i in now}
            for key, use in uses.items():
                if key[0] == "middle":
                    use[4].update(growth)
            for i in now:
                now[i] = start[i] + growth[i] * (NB - 2)
            add("last", in_order(LAST), lambda i: 0)
            add("epilogue", EPILOGUE, lambda i: 0)
            return uses

        uses = plan()

        class Use:

            def __init__(self, part, kind, arg, b):
                self.bank, self.before, self.filled, self.after, self.growth = uses[part, kind, arg]
                self.b = b
                self.ps = bank[self.bank]

            def value(self, count, i):
                grow = self.growth[i]
                return self.b * grow + (count - grow) if grow else count

            def wait_free(self, pe):
                for e, count in self.before:
                    pe.wait_ge(read[self.bank, e], self.value(count, (self.bank, e)))

            def wait_full(self, eng):
                eng.wait_ge(full[self.bank], self.value(self.filled, ("full", self.bank)))

            def wait_read(self, eng, e):
                eng.wait_ge(read[self.bank, e], self.value(self.after[e], (self.bank, e)))

            @property
            def is_full(self):
                return full[self.bank]

            def read_by(self, e):
                return read[self.bank, e]

        def done(b, s, more=0):
            return b * NP + (s + 1 + more)

        def hold(eng, semaphore, count, passed):
            eng.wait_ge(semaphore, count)
            eng.sem_inc(passed, 1)

        def after(b, s, n):
            return (b, s + n) if s + n < NP else (b + 1, s + n - NP)

        def run(eng, prologue, step, epilogue):
            def steps(of, left=None):
                for b, s, events, part in of:
                    ahead, behind = ([(kind, arg, part, b) for kind, arg, _ in some] for some in events)
                    leave = behind.pop() if behind and behind[-1][0] in DEFERRED else None
                    step(b, s, ahead, behind, leave, left, part)
                    left = leave
                return left

            def left_by_step_0(b):
                kind, arg, _ = MIDDLE[0][1][-1]
                return kind, arg, "middle", b

            prologue()
            steps([(0, s, FIRST[s], "first") for s in range(NP)] + [(1, 0, MIDDLE[0], "middle")])
            with eng.Fori(1, NB - 1) as b:
                steps([(b, s, MIDDLE[s], "middle") for s in range(1, NP)] + [(b + 1, 0, MIDDLE[0], "middle")],
                      left_by_step_0(b))
            left = steps([(NB - 1, s, LAST[s], "last") for s in range(1, NP)], left_by_step_0(NB - 1))
            assert left is None
            epilogue([(kind, arg, "epilogue", NB) for kind, arg, _ in EPILOGUE])

        def with_last(behind, leave):
            return behind + [leave] * bool(leave)

        def follows(b, s, n):
            return not (isinstance(b, int) and b * NP + s + n >= NB * NP)

        a_of = {n: i for i, n in enumerate(LOADS)}

        def slot_of(kind, arg):
            return stage[:, a_of[kind, arg] % SLOTS, :], slot_loaded[a_of[kind, arg] % SLOTS]

        N_DMAS = {"A": 4, "B": 2, "F": 1}

        def slot_count(kind, arg):
            n = a_of[kind, arg]
            return 16 * sum(N_DMAS[k] for k, _ in LOADS[n % SLOTS:n + 1:SLOTS])

        block = ctx.enter_context(nc.Block())

        @block.sync
        def _(sp):
            def load_x(b):
                sp.dma_start(x_in[:, :, :], x[b].rearrange("(t p) c -> p t c", p=P)).then_inc(x_in_loaded, 16)

            def load_res(b):
                sp.dma_start(x_res[:, :, :], x[b].rearrange("(t p) c -> p t c", p=P)).then_inc(x_res_loaded, 16)

            def store_y(b):
                sp.wait_ge(y_ready, b + 1)
                sp.dma_start(out[b].rearrange("(t p) c -> p t c", p=P), y[:, :, :]).then_inc(y_free, 16)

            def load_weights(n):
                kind, i = LOADS[n]
                to, loaded = slot_of(kind, i)
                if n >= SLOTS:
                    k, j = LOADS[n - SLOTS]
                    part = "prologue" if ("prologue", k, j) in uses else "first"
                    Use(part, k, j, 0).wait_full(sp)
                if kind == "A":
                    heads = wq.rearrange("(h r) c -> r h c", r=DQ)[:, 2 * i:2 * i + 2, :]
                    kv = wkvb.rearrange("(h r) c -> r h c", r=NOPE + DV)[0:NOPE, 2 * i:2 * i + 2, :]
                    sp.dma_start(to[:, 0:512].rearrange("p (h c) -> p h c", h=2), heads[0:NOPE]).then_inc(loaded, 16)
                    sp.dma_start(to[:, 512:640].rearrange("p (h c) -> p h c", h=2), kv).then_inc(loaded, 16)
                    for h in range(2):
                        sp.dma_start(to[h * ROPE:(h + 1) * ROPE, 640:896], heads[NOPE:DQ, h, :]).then_inc(loaded, 16)
                elif kind == "B":
                    kv = wkvb.rearrange("(h r) c -> r h c", r=NOPE + DV)[NOPE:NOPE + DV, 2 * i:2 * i + 2, :]
                    cols = wo[:, 2 * i * DV:2 * (i + 1) * DV].rearrange("(o p) c -> p o c", p=P)
                    sp.dma_start(to[:, 0:512].rearrange("p (o c) -> p o c", o=2), cols).then_inc(loaded, 16)
                    sp.dma_start(to[:, 512:640].rearrange("p (h c) -> p h c", h=2), kv).then_inc(loaded, 16)
                else:
                    which, jj = divmod(i, 4)
                    if which < 2:
                        w = (w_gate, w_up)[which].rearrange("(j p) c -> p j c", p=P)[:, 2 * jj:2 * jj + 2, :]
                    else:
                        w = w_down[:, 2 * jj * P:2 * (jj + 1) * P].rearrange("(o p) c -> p o c", p=P)
                    sp.dma_start(to[:, 0:512].rearrange("p (j c) -> p j c", j=2), w).then_inc(loaded, 16)

            load_x(0)
            sp.dma_start(wkva_raw[:, :], wkva).then_inc(wkva_loaded, 16)
            for n in range(len(LOADS)):
                load_weights(n)
                if n == 1:
                    Use("prologue", "XT", 0, 0).wait_full(sp)
                    load_x(1)
                if n == 5:
                    load_res(0)
            Use("first", "XT", 1, 0).wait_full(sp)
            load_x(2)
            with sp.Fori(1, NB - 2) as b:
                Use("middle", "OUT", 1, b).wait_read(sp, "dve")
                load_res(b)
                Use("middle", "XT", 1, b).wait_full(sp)
                load_x(b + 2)
                store_y(b - 1)
            Use("middle", "OUT", 1, NB - 2).wait_read(sp, "dve")
            load_res(NB - 2)
            store_y(NB - 3)
            Use("last", "OUT", 1, NB - 1).wait_read(sp, "dve")
            load_res(NB - 1)
            store_y(NB - 2)
            store_y(NB - 1)
            sp.wait_ge(y_free, 16 * (NB + 1))

        @block.tensor
        def _(pe):
            def three(ps, w_hi, w_lo, m_hi, m_lo, start, stop):
                nc.tensor.matmul(ps, w_hi, m_hi, start=start, stop=False)
                nc.tensor.matmul(ps, w_hi, m_lo, start=False, stop=False)
                return nc.tensor.matmul(ps, w_lo, m_hi, start=False, stop=stop)

            def transposes(b, s):
                for h in range(2):
                    pe.wait_ge(prob_ready[h], done(b, s))
                    for i in range(3):
                        last = nc.tensor.transpose(t_ps[h][:, i * P:(i + 1) * P], prob[:, h, i * P:(i + 1) * P],
                                                   ident[:, :])
                    last.then_inc(t_done[h], 1)

            def queries(b, s):
                if s == 0:
                    pe.wait_ge(xt_hi_ready, b + 1)
                    pe.wait_ge(xt_lo_ready, b + 1)
                if isinstance(b, int) and b == 0:
                    part = "prologue" if s < 3 else "first"
                    Use(part, "A", s, 0).wait_read(pe, "dve")
                for h in range(2):
                    n = 2 * s + h
                    for c in range(NC):
                        last = three(q_ps[:, h, :], a_hi[:, c, n, :], a_lo[:, c, n, :], xt_hi[:, c, :],
                                     xt_lo[:, c, :], c == 0, c == NC - 1)
                last.then_inc(q_done, 1)

            def scores(b, s):
                pe.wait_ge(q_lo_ready, done(b, s))
                i = s % 2
                for h in range(2):
                    nc.tensor.matmul(s_ps[h][:, 0:P], q0[:, i, h, :], kt[:, :], start=True, stop=True)
                    three(s_ps[h][:, P:3 * P], q1_hi[:, i, h, :], q1_lo[:, i, h, :], kt_hi[:, :], kt_lo[:, :],
                          True, True).then_inc(s_done[h], 1)

            def values(b, s):
                for h in range(2):
                    pe.wait_ge(pt_lo_ready[h], done(b, s))
                if s == 0:
                    pe.wait_ge(c_parts_ready, b + 1)
                if not (isinstance(b, int) and b == 0 and s == 0):
                    pe.wait_ge(o_sum_ready, done(b, s, -1))
                for k in range(NT):
                    cols = slice(0, S) if k == 0 else slice(S, S + P)
                    for pt in (pt_hi, pt_lo):
                        last = nc.tensor.matmul(o_ps[:, :, k * P:S], c_parts[:, k, :, :], pt[:, :, cols],
                                                start=(k == 0 and pt is pt_hi), stop=(k == 1 and pt is pt_lo))
                last.then_inc(o_done, 1)

            def project(b, ps, t, pairs):
                cols = slice(t * P, (t + 1) * P)
                for p in pairs:
                    if t == 0 and p >= NP // 2:
                        pe.wait_ge(ot_ready, done(b - 1, p))
                    last = three(ps[:, 0:HID], ot_hi[:, p, cols], ot_lo[:, p, cols], b_hi[:, p, :],
                                 b_lo[:, p, :], p == 0, p == NP - 1)
                return last

            def down(b, ps, t, chunks):
                cols = slice(t * P, (t + 1) * P)
                for j in chunks:
                    if t == 0:
                        pe.wait_ge(h_ready, (b - 1) * NJ + (j + 1))
                    last = three(ps[:, 0:HID], h_hi[:, j, cols], h_lo[:, j, cols], ff_hi[2][:, j, :],
                                 ff_lo[2][:, j, :], j == 0, j == NJ - 1)
                return last

            def event(kind, arg, part, b):
                if kind in ("CNORM", "XSPLIT"):
                    return
                if kind == "OUTA":
                    for t in range(2):
                        Use(part, "OUT", t, b).wait_free(pe)
                    pe.wait_ge(ot_ready, done(b - 1, NP // 2 - 1))
                    for t in range(2):
                        last = project(b, Use(part, "OUT", t, b).ps, t, range(NP // 2))
                    last.then_inc(out_half, 1)
                    return
                if kind == "DNA":
                    use = Use(part, "DN", arg, b)
                    use.wait_free(pe)
                    down(b, use.ps, arg, range(AHEAD[part]))
                    return
                use = Use(part, kind, arg, b)
                ps = use.ps
                if kind != "OUT" and (kind != "DN" or AHEAD[part] == 0):
                    use.wait_free(pe)
                if kind == "XT":
                    nb = b + arg
                    pe.wait_ge(x_in_loaded, (nb + 1) * 16)
                    if part == "prologue":
                        pe.wait_ge(ident_ready, 1)
                    for c in range(NC):
                        for t in range(NT):
                            last = nc.tensor.transpose(ps[:, c * S + t * P:c * S + (t + 1) * P],
                                                       x_in[:, t, c * P:(c + 1) * P], ident[:, :])
                elif kind == "WKVA":
                    pe.wait_ge(wkva_loaded, 16)
                    pe.wait_ge(rope_ready, 2)
                    for c in range(NC):
                        last = nc.tensor.matmul(ps[:, c * P:(c + 1) * P], wkva_raw[:, c * P:(c + 1) * P],
                                                kfold[:, :, :], start=True, stop=True)
                elif kind == "CKV":
                    Use(part, "XT", arg, b).wait_read(pe, "act")
                    if part == "prologue":
                        Use(part, "WKVA", 0, 0).wait_read(pe, "dve")
                    for t in range(NT):
                        for c in range(NC):
                            last = nc.tensor.matmul(ps[:, t * P:(t + 1) * P], xt[:, c, t * P:(t + 1) * P],
                                                    wkvat[:, c, :], start=(c == 0), stop=(c == NC - 1))
                elif kind == "KT":
                    pe.wait_ge(c_ready, b + arg + 1)
                    for t in range(NT):
                        last = nc.tensor.transpose(ps[:, t * P:(t + 1) * P], ckv[:, t, :], ident[:, :])
                elif kind == "A":
                    w, loaded = slot_of("A", arg)
                    pe.wait_ge(loaded, slot_count("A", arg))
                    for c in range(NC):
                        for h in range(2):
                            nc.tensor.matmul(ps[:, c * S + h * LORA:c * S + h * LORA + P],
                                             w[:, h * HID + c * P:h * HID + (c + 1) * P],
                                             w[:, 512 + h * LORA:512 + h * LORA + P], start=True, stop=True)
                        last = nc.tensor.matmul(ps[:, c * S + P:(c + 1) * S], w[:, 640 + c * P:640 + (c + 1) * P],
                                                ropet[:, :, :], start=True, stop=True)
                elif kind == "WOT":
                    w, loaded = slot_of("B", arg)
                    pe.wait_ge(loaded, slot_count("B", arg))
                    for h in range(2):
                        for o in range(NC):
                            last = nc.tensor.transpose(ps[:, h * HID + o * P:h * HID + (o + 1) * P],
                                                       w[:, o * 256 + h * P:o * 256 + (h + 1) * P], ident[:, :])
                elif kind == "B":
                    w, _ = slot_of("B", arg)
                    Use(part, "WOT", arg, 0).wait_read(pe, "dve")
                    for h in range(2):
                        last = nc.tensor.matmul(ps[:, h * HID:(h + 1) * HID], w[:, 512:640], wot[:, h, :],
                                                start=True, stop=True)
                elif kind == "F":
                    w, loaded = slot_of("F", arg)
                    pe.wait_ge(loaded, slot_count("F", arg))
                    for j in range(2):
                        for c in range(2):
                            at = c * 256 + j * P if arg < 8 else j * 256 + c * P
                            src = j * 256 + c * P if arg < 8 else c * 256 + j * P
                            last = nc.tensor.transpose(ps[:, at:at + P], w[:, src:src + P], ident[:, :])
                elif kind == "X1T":
                    pe.wait_ge(x1_ready, b)
                    for c in range(NC):
                        for t in range(NT):
                            last = nc.tensor.transpose(ps[:, c * S + t * P:c * S + (t + 1) * P],
                                                       x1[:, t, c * P:(c + 1) * P], ident[:, :])
                elif kind == "GU":
                    if arg == 0:
                        Use(part, "X1T", 0, b).wait_read(pe, "dve")
                    cols = slice(arg * P, (arg + 1) * P)
                    for g in range(2):
                        for c in range(NC):
                            last = three(ps[:, g * S:(g + 1) * S], ff_hi[g][:, c, cols], ff_lo[g][:, c, cols],
                                         x1t_hi[:, c, :], x1t_lo[:, c, :], c == 0, c == NC - 1)
                elif kind == "OUT":
                    last = project(b, ps, arg, range(NP // 2, NP))
                elif kind == "DN":
                    last = down(b, ps, arg, range(AHEAD[part], NJ))
                last.then_inc(use.is_full, 1)

            def prologue():
                event("XT", 0, "prologue", 0)
                for kind, arg in (("WKVA", 0), ("CKV", 0), ("A", 0), ("KT", 0), ("A", 1)):
                    event(kind, arg, "prologue", 0)
                queries(0, 0)
                event("A", 2, "prologue", 0)
                Use("prologue", "KT", 0, 0).wait_read(pe, "dve")
                scores(0, 0)
                queries(0, 1)
                for j in range(2):
                    event("F", j, "prologue", 0)

            def step(b, s, ahead, behind, leave, left, part):
                transposes(b, s)
                if follows(b, s, 1):
                    if s == NP - 1:
                        Use(part, "KT", 1, b).wait_read(pe, "dve")
                    scores(*after(b, s, 1))
                if follows(b, s, 2):
                    queries(*after(b, s, 2))
                for e in ahead:
                    event(*e)
                values(b, s)
                for e in with_last(behind, leave):
                    event(*e)

            def epilogue(events):
                for e in events:
                    event(*e)

            run(pe, prologue, step, epilogue)

        @block.scalar
        def _(act):
            def copy(to, of):
                return nc.scalar.activation(to, of, ACT.Copy)

            def pt_high(b, s, h):
                act.wait_ge(t_done[h], done(b, s))
                copy(pt_hi[:, h, :], t_ps[h][:, 0:3 * P]).then_inc(pt_hi_ready[h], 1)

            def q_parts(b, s):
                act.wait_ge(q_done, done(b, s))
                copy(q0[:, s % 2, :, :], q_ps[:, :, 0:P])
                copy(q1_hi[:, s % 2, :, :], q_ps[:, :, P:S]).then_inc(q_act_ready, 1)

            def exps(b, s, h):
                act.wait_ge(max_ready[h], done(b, s))
                for t, cols in ((0, slice(0, P)), (1, slice(P, 3 * P))):
                    last = nc.scalar.activation(prob[:, h, cols], prob[:, h, cols], ACT.Exp,
                                                bias=nmax[:, h, t:t + 1], scale=-1.0,
                                                accum_out=rowsum[:, h, t:t + 1])
                last.then_inc(exp_ready[h], 1)

            def o_low_half(b, s):
                act.wait_ge(o_done, done(b, s))
                copy(o_low[:, :, :], o_ps[LORA:P, :, :]).then_inc(o_low_ready, 1)

            def event(kind, arg, part, b):
                if kind == "XSPLIT":
                    if part != "prologue":
                        act.wait_ge(q_done, done(b, NP - 1))
                    copy(xt_hi[:, :, :], xt[:, :, :]).then_inc(xt_hi_ready, 1)
                    return
                if kind not in READERS or "act" not in READERS[kind]:
                    return
                use = Use(part, kind, arg, b)
                ps = use.ps
                use.wait_full(act)
                if kind == "XT":
                    last = copy(xt[:, :, :], ps[:, :])
                elif kind == "CKV":
                    copy(ckv[:, :, :], ps[:, 0:NT * P]).then_inc(use.read_by("act"), 1)
                    use.wait_read(act, "act")
                    for t in range(NT):
                        last = nc.scalar.activation(squares[:, t, :], ckv[:, t, 0:LORA], ACT.Square,
                                                    accum_out=ssq[:, t:t + 1])
                    last.then_inc(ssq_ready, 1)
                    return
                elif kind == "KT":
                    copy(kt[:, :], ps[:, 0:P])
                    last = copy(kt_hi[:, :], ps[:, 0:S])
                elif kind == "A":
                    for c in range(NC):
                        last = copy(a_hi[:, c, 2 * arg:2 * arg + 2, :].rearrange("p h (k d) -> p k h d", k=2),
                                    ps[:, c * S:(c + 1) * S].rearrange("p (k h d) -> p k h d", k=2, h=2))
                elif kind == "B":
                    for h in range(2):
                        rows = slice(h * LORA, (h + 1) * LORA)
                        last = copy(b_hi[rows, arg, :], ps[rows, h * HID:(h + 1) * HID])
                elif kind == "F":
                    which, jj = divmod(arg, 4)
                    if which < 2:
                        last = copy(ff_hi[which][:, :, jj * 256:(jj + 1) * 256],
                                    ps[:, :].rearrange("p (c j) -> p c j", c=2))
                    else:
                        last = copy(ff_hi[2][:, 2 * jj:2 * jj + 2, :], ps[:, :])
                elif kind == "X1T":
                    last = copy(x1t_hi[:, :, :], ps[:, :])
                elif kind == "GU":
                    if arg >= 2:
                        Use(part, "GU", arg - 2, b).wait_read(act, "dve")
                    last = nc.scalar.activation(act_g[:, arg % 2, :], ps[:, 0:S], ACT.Tanh, scale=0.5)
                last.then_inc(use.read_by("act"), 1)

            def prologue():
                for to, of in ((cosb, cos), (sinb, sin)):
                    act.dma_start(to[:, :], of.partition_broadcast(P)).then_inc(rope_loaded, 16)
                act.dma_start(normw[:, :], norm_w.rearrange("(a n) -> a n", a=1).partition_broadcast(P))\
                   .then_inc(normw_loaded, 16)
                event("XT", 0, "prologue", 0)
                Use("prologue", "XT", 0, 0).wait_read(act, "act")
                event("XSPLIT", 0, "prologue", 0)
                for kind, arg in (("CKV", 0), ("A", 0), ("KT", 0), ("A", 1)):
                    event(kind, arg, "prologue", 0)
                q_parts(0, 0)
                event("A", 2, "prologue", 0)
                for h in range(2):
                    exps(0, 0, h)
                q_parts(0, 1)
                for j in range(2):
                    event("F", j, "prologue", 0)

            def step(b, s, ahead, behind, leave, left, part):
                for h in range(2):
                    pt_high(b, s, h)
                if follows(b, s, 1):
                    for h in range(2):
                        exps(*after(b, s, 1), h)
                if follows(b, s, 2):
                    q_parts(*after(b, s, 2))
                for e in ahead:
                    event(*e)
                o_low_half(b, s)
                for e in with_last(behind, leave):
                    event(*e)

            def epilogue(events):
                for e in events:
                    event(*e)

            run(act, prologue, step, epilogue)

        @block.vector
        def _(dve):
            tt, stt = nc.vector.tensor_tensor, nc.vector.scalar_tensor_tensor

            def low(to, of, high):
                return tt(to, of, high.bitcast(F32), ALU.subtract)

            def pt_low(b, s, h):
                dve.wait_ge(pt_hi_ready[h], done(b, s))
                low(pt_lo[:, h, :], t_ps[h][:, 0:3 * P], pt_hi[:, h, :]).then_inc(pt_lo_ready[h], 1)

            def maxima(b, s, h):
                hold(dve, s_done[h], done(b, s), dve_passed)
                for t, cols in ((0, slice(0, P)), (1, slice(P, 3 * P))):
                    last = nc.vector.tensor_tensor_reduce(
                        out=prob[:, h, cols], in0=s_ps[h][:, cols], in1=mask[:, (1 - t) * P:2 * P], scale=-SCALE,
                        scalar=TOP, op0=ALU.add, op1=ALU.min, accum_out=nmax[:, h, t:t + 1])
                last.then_inc(max_ready[h], 1)

            def row_reciprocals(b, s, h):
                dve.wait_ge(exp_ready[h], done(b, s))
                nc.vector.reciprocal(rrow[:, h, :], rowsum[:, h, :]).then_inc(rrow_ready[h], 1)

            def q_low(b, s):
                dve.wait_ge(q_act_ready, done(b, s))
                low(q1_lo[:, s % 2, :, :], q_ps[:, :, P:S], q1_hi[:, s % 2, :, :]).then_inc(q_lo_ready, 1)

            def o_add(b, s):
                dve.wait_ge(o_low_ready, done(b, s))
                if not (isinstance(b, int) and b == 0 and s == 0):
                    dve.wait_ge(ot_ready, done(b, s, -1))
                for h in range(2):
                    last = tt(o_sum[h * LORA:(h + 1) * LORA, :], o_ps[0:LORA, h, :], o_low[:, h, :], ALU.add)
                last.then_inc(o_sum_ready, 1)

            def ln_sum(n, residual, t, use):
                use.wait_full(dve)
                tt(res[:, t, :], use.ps[:, 0:HID], residual[:, t, :], ALU.add).then_inc(use.read_by("dve"), 1)
                use.wait_read(dve, "dve")
                last = nc.vector.bn_stats(stats[:, t, :], res[:, t, :])
                if t < NT - 1:
                    return
                last.then_inc(ln_chain, 1)
                hold(dve, ln_chain, n * 2 + 1, dve_passed)
                for t in range(NT):
                    last = nc.vector.bn_aggr(moments[:, t, :], stats[:, t, :])
                last.then_inc(ln_chain, 1)
                dve.wait_ge(ln_chain, n * 2 + 2)
                nc.vector.tensor_scalar(vareps[:, :], moments[:, :, 1], LN_EPS, None, ALU.add).then_inc(vareps_ready, 1)

            def ln_scale(n, to, ready):
                dve.wait_ge(rstd_ready, n + 1)
                for t in range(NT):
                    last = nc.vector.tensor_scalar(to[:, t, :], res[:, t, :], moments[:, t, 0:1], rstd[:, t:t + 1],
                                                   ALU.subtract, ALU.mult)
                last.then_inc(ready, 1)

            def ln2_scale(f):
                dve.wait_ge(y_free, f * 16 + 16)
                ln_scale(f * 2 + 1, y, y_ready)

            def event(kind, arg, part, b):
                if kind == "XSPLIT":
                    dve.wait_ge(xt_hi_ready, b + arg + 1)
                    low(xt_lo[:, :, :], xt[:, :, :], xt_hi[:, :, :]).then_inc(xt_lo_ready, 1)
                elif kind == "CNORM":
                    if part == "prologue":
                        dve.wait_ge(normw_loaded, 16)
                    dve.wait_ge(rms_ready, b + arg + 1)
                    for t in range(NT):
                        last = stt(ckv[:, t, 0:LORA], ckv[:, t, 0:LORA], rms[:, t:t + 1], normw[:, :], ALU.mult,
                                   ALU.mult)
                    last.then_inc(c_ready, 1)
                elif kind == "CKV":
                    dve.wait_ge(ssq_ready, b + arg + 1)
                    nc.vector.tensor_scalar(msq[:, :], ssq[:, :], 1.0 / LORA, RMS_EPS, ALU.mult, ALU.add)\
                      .then_inc(msq_ready, 1)
                elif kind == "OUT":
                    if arg == 0:
                        dve.wait_ge(x_res_loaded, b * 16)
                        if part == "epilogue":
                            dve.wait_ge(y_ready, NB - 1)
                    ln_sum((b - 1) * 2, x_res, arg, Use(part, kind, arg, b))
                elif kind == "DN":
                    if arg == 0:
                        dve.wait_ge(x1_ready, b)
                    ln_sum((b - 1) * 2 + 1, x1, arg, Use(part, kind, arg, b))
                if kind not in ("WKVA", "WOT", "A", "KT", "B", "F", "X1T", "GU"):
                    return
                use = Use(part, kind, arg, b)
                ps = use.ps
                if kind == "WKVA":
                    use.wait_full(dve)
                    last = nc.vector.tensor_copy(wkvat[:, :, :], ps[:, 0:NC * P])
                elif kind == "WOT":
                    use.wait_full(dve)
                    last = nc.vector.tensor_copy(wot[:, :, :], ps[:, :])
                else:
                    use.wait_read(dve, "act")
                if kind == "KT":
                    last = low(kt_lo[:, :], ps[:, 0:S], kt_hi[:, :])
                elif kind == "A":
                    for c in range(NC):
                        last = low(a_lo[:, c, 2 * arg:2 * arg + 2, :].rearrange("p h (k d) -> p k h d", k=2),
                                   ps[:, c * S:(c + 1) * S].rearrange("p (k h d) -> p k h d", k=2, h=2),
                                   a_hi[:, c, 2 * arg:2 * arg + 2, :].rearrange("p h (k d) -> p k h d", k=2))
                elif kind == "B":
                    for h in range(2):
                        rows = slice(h * LORA, (h + 1) * LORA)
                        last = low(b_lo[rows, arg, :], ps[rows, h * HID:(h + 1) * HID], b_hi[rows, arg, :])
                elif kind == "F":
                    which, jj = divmod(arg, 4)
                    if which < 2:
                        cols = slice(jj * 256, (jj + 1) * 256)
                        last = low(ff_lo[which][:, :, cols], ps[:, :].rearrange("p (c j) -> p c j", c=2),
                                   ff_hi[which][:, :, cols])
                    else:
                        last = low(ff_lo[2][:, 2 * jj:2 * jj + 2, :], ps[:, :].rearrange("p (j c) -> p j c", j=2),
                                   ff_hi[2][:, 2 * jj:2 * jj + 2, :])
                elif kind == "X1T":
                    last = low(x1t_lo[:, :, :], ps[:, :].rearrange("p (c s) -> p c s", c=NC), x1t_hi[:, :, :])
                elif kind == "GU":
                    i = arg % 2
                    stt(act_g[:, i, :], act_g[:, i, :], 1.0, ps[:, 0:S], ALU.add, ALU.mult).then_inc(gated, 1)
                    dve.wait_ge(gated, (b - 1) * NJ + (arg + 1))
                    if arg >= 2:
                        dve.wait_ge(h_ready, (b - 1) * NJ + (arg - 1))
                    last = stt(h_sum[:, i, :], act_g[:, i, :], 0.5, ps[:, S:2 * S], ALU.mult, ALU.mult)
                last.then_inc(use.read_by("dve"), 1)

            def prologue():
                dve.wait_ge(rope_loaded, 16 * 2)
                dve.wait_ge(ident_ready, 1)
                dve.wait_ge(rot_ready, 2)
                for k in range(2):
                    tt(rot[:, k, :], rot[:, k, :], sinb[:, :], ALU.mult)
                    last = tt(ropet[:, k, :], cosb[:, :], ident[:, k * ROPE:(k + 1) * ROPE], ALU.mult)
                last.then_inc(rope_chain, 1)
                dve.wait_ge(rope_chain, 1)
                tt(ropet[:, :, :], ropet[:, :, :], rot[:, :, :], ALU.add).then_inc(rope_ready, 1)
                nc.vector.tensor_copy(kfold[:, 0, :], ident[:, 0:LORA])
                dve.wait_ge(rope_ready, 1)
                nc.vector.tensor_copy(kfold[:, 1, :], ropet[:, 1, :]).then_inc(rope_ready, 1)
                event("WKVA", 0, "prologue", 0)
                for kind, arg in (("XSPLIT", 0), ("CKV", 0), ("CNORM", 0), ("A", 0), ("KT", 0), ("A", 1)):
                    event(kind, arg, "prologue", 0)
                q_low(0, 0)
                event("A", 2, "prologue", 0)
                dve.wait_ge(mask_ready, 1)
                for h in range(2):
                    maxima(0, 0, h)
                for h in range(2):
                    row_reciprocals(0, 0, h)
                q_low(0, 1)
                for j in range(2):
                    event("F", j, "prologue", 0)

            def step(b, s, ahead, behind, leave, left, part):
                pt_low(b, s, 0)
                if follows(b, s, 1):
                    for h in range(2):
                        maxima(*after(b, s, 1), h)
                pt_low(b, s, 1)
                if left:
                    event(*left)
                if s == 0 and not isinstance(b, int):
                    ln2_scale(b - 2)
                if s == 2 and part != "first":
                    ln_scale((b - 1) * 2, x1, x1_ready)
                if follows(b, s, 1):
                    row_reciprocals(*after(b, s, 1), 0)
                for e in ahead:
                    if e[0] == "WOT":
                        event(*e)
                if follows(b, s, 1):
                    row_reciprocals(*after(b, s, 1), 1)
                if follows(b, s, 2):
                    q_low(*after(b, s, 2))
                for e in ahead:
                    if e[0] != "WOT":
                        event(*e)
                o_add(b, s)
                for e in behind:
                    event(*e)

            def epilogue(events):
                ln2_scale(NB - 2)
                for e in events:
                    event(*e)
                    if e[:2] == ("OUT", NT - 1):
                        ln_scale((NB - 1) * 2, x1, x1_ready)
                ln2_scale(NB - 1)

            run(dve, prologue, step, epilogue)

        @block.gpsimd
        def _(pool):
            def keep(to, of):
                return nc.gpsimd.tensor_scalar(to, of, 1.0, 1.0, ALU.mult, ALU.mult)

            def normalise(b, s, h):
                hold(pool, rrow_ready[h], done(b, s), pool_passed)
                for t, cols in ((0, slice(0, P)), (1, slice(P, 3 * P))):
                    last = nc.gpsimd.tensor_scalar(prob[:, h, cols], prob[:, h, cols], rrow[:, h, t:t + 1], 1.0,
                                                   ALU.mult, ALU.mult)
                last.then_inc(prob_ready[h], 1)

            def o_split(b, s):
                pool.wait_ge(o_sum_ready, done(b, s))
                if not (isinstance(b, int) and b == 0):
                    if s == 0:
                        pool.wait_ge(out_half, b)
                    if s == NP // 2:
                        Use("middle", "OUT", 1, b).wait_full(pool)
                pool.sem_inc(pool_passed, 1)
                keep(ot_hi[:, s, :], o_sum[:, :]).then_inc(ot_hi_ready, 1)
                pool.wait_ge(ot_hi_ready, done(b, s))
                nc.gpsimd.tensor_tensor(ot_lo[:, s, :], o_sum[:, :], ot_hi[:, s, :].bitcast(F32), ALU.subtract)\
                    .then_inc(ot_ready, 1)

            def c_split(nb):
                pool.wait_ge(c_ready, nb + 1)
                if not isinstance(nb, int) or nb > 0:
                    pool.wait_ge(o_done, nb * NP)
                pool.sem_inc(pool_passed, 1)
                keep(c_parts[:, :, 0, :], ckv[:, :, 0:LORA]).then_inc(c_hi_ready, 1)
                pool.wait_ge(c_hi_ready, nb + 1)
                nc.gpsimd.tensor_tensor(c_parts[:, :, 1, :], ckv[:, :, 0:LORA], c_parts[:, :, 0, :].bitcast(F32),
                                        ALU.subtract).then_inc(c_parts_ready, 1)

            def event(kind, arg, part, b):
                if kind == "CKV":
                    pool.wait_ge(msq_ready, b + arg + 1)
                    nc.gpsimd.tensor_tensor(rms[:, :], msq[:, :], mhalf[:, :], ALU.pow).then_inc(rms_ready, 1)
                elif kind in ("OUT", "DN") and arg == NT - 1:
                    n = (b - 1) * 2 + (kind == "DN")
                    pool.wait_ge(vareps_ready, n + 1)
                    nc.gpsimd.tensor_tensor(rstd[:, :], vareps[:, :], mhalf[:, :], ALU.pow).then_inc(rstd_ready, 1)
                elif kind == "GU":
                    Use(part, kind, arg, b).wait_read(pool, "dve")
                    pool.sem_inc(pool_passed, 1)
                    keep(h_hi[:, arg, :], h_sum[:, arg % 2, :]).then_inc(h_hi_ready, 1)
                    pool.wait_ge(h_hi_ready, (b - 1) * NJ + (arg + 1))
                    nc.gpsimd.tensor_tensor(h_lo[:, arg, :], h_sum[:, arg % 2, :], h_hi[:, arg, :].bitcast(F32),
                                            ALU.subtract).then_inc(h_ready, 1)

            def prologue():
                nc.gpsimd.memset(ident[:, :], 0.0).then_inc(zeroed, 1)
                nc.gpsimd.memset(rot[:, :, :], 0.0).then_inc(zeroed, 1)
                nc.gpsimd.memset(mask[:, :], 0.0).then_inc(zeroed, 1)
                nc.gpsimd.memset(mhalf[:, :], -0.5)
                nc.gpsimd.memset(y[:, :, :], 0.0).then_inc(y_free, 16)
                pool.wait_ge(zeroed, 3)
                nc.gpsimd.affine_select(out=ident[:, :], in_=ident[:, :], compare_op=ALU.not_equal, fill=1.0, base=0,
                                        pattern=[[-1, P]], channel_multiplier=1).then_inc(ident_ready, 1)
                half = ROPE // 2
                for k, (sign, base) in enumerate(((-1.0, -half), (1.0, 0))):
                    v = rot[:, :, k * half:(k + 1) * half]
                    nc.gpsimd.affine_select(out=v, in_=v, compare_op=ALU.not_equal, fill=sign, base=base,
                                            pattern=[[-ROPE, 2], [-1, half]], channel_multiplier=1)\
                        .then_inc(rot_ready, 1)
                nc.gpsimd.affine_select(out=mask[:, P:2 * P], in_=mask[:, P:2 * P], compare_op=ALU.is_ge, fill=MASKED,
                                        base=0, pattern=[[-1, P]], channel_multiplier=1).then_inc(mask_ready, 1)
                event("CKV", 0, "prologue", 0)
                c_split(0)
                for h in range(2):
                    normalise(0, 0, h)

            def step(b, s, ahead, behind, leave, left, part):
                if follows(b, s, 1):
                    for h in range(2):
                        normalise(*after(b, s, 1), h)
                if left:
                    event(*left)
                if s == NP - 1 and follows(b, s, 1):
                    c_split(b + 1)
                for e in ahead:
                    event(*e)
                o_split(b, s)
                for e in behind:
                    event(*e)

            def epilogue(events):
                for e in events:
                    event(*e)

            run(pool, prologue, step, epilogue)


_INS = ["L0_attn_hidden_states", "L0_attn_Wq", "L0_attn_Wkva", "L0_attn_kv_a_norm_weight", "L0_attn_Wkvb",
        "L0_attn_Wo", "L0_attn_cos", "L0_attn_sin", "L0_ffn_w_gate", "L0_ffn_w_up", "L0_ffn_w_down"]


def kernel(**inputs):
    import numpy as _np
    import concourse.bacc as _bacc
    from concourse import mybir as _mybir
    from concourse.bass_utils import run_bass_kernel_spmd as _run

    nc = _bacc.Bacc("TRN2", target_bir_lowering=False, num_devices=1)
    arrays, args = {}, []
    for name in _INS:
        a = _np.ascontiguousarray(inputs[name])
        arrays[f"in_{name}_dram"] = a
        args.append(nc.dram_tensor(f"in_{name}_dram", a.shape, _mybir.dt.from_np(a.dtype), kind="ExternalInput").ap())
    out = nc.dram_tensor("out_dram", (NB, S, HID), _mybir.dt.float32, kind="ExternalOutput").ap()
    layer(nc, *args, out)
    return _run(nc, [arrays], core_ids=[0]).results[0]["out_dram"]
```

```python
from contextlib import ExitStack

import concourse.bass as bass
from concourse import mybir
from concourse.alu_op_type import AluOpType as ALU

F32 = mybir.dt.float32
F32R = mybir.dt.float32r
ACT = mybir.ActivationFunctionType

P = 128
NB, S, HID = 8, 256, 256
NH, NOPE, ROPE, DV, LORA = 16, 128, 64, 128, 64
DQ = NOPE + ROPE
FF = 1024
NT = S // P
NC = HID // P
NP = NH // 2
NJ = FF // P
SCALE = float(DQ) ** -0.5
RMS_EPS = 1e-6
LN_EPS = 1e-5
MASKED = -3.0e38
TOP = 3.4e38
SLOTS = 6
SLOT = 896

READERS = {"WKVA": ("dve",), "XT": ("act",), "CKV": ("act",), "A": ("act", "dve"), "KT": ("act", "dve"),
           "WOT": ("dve",), "B": ("act", "dve"), "F": ("act", "dve"), "OUT": ("dve",), "X1T": ("act", "dve"),
           "X1TILE": ("act", "dve"), "GU": ("act", "dve"), "DN": ("dve",)}

PROLOGUE = [("WKVA", 0, "G"), ("XT", 0, "Y"), ("CKV", 0, "Y"), ("A", 0, "G"), ("A", 1, "Y"), ("KT", 0, "S"),
            ("A", 2, "G"), ("F", 0, "Y"), ("F", 1, "G")]
FIRST = [
    ([("WOT", 0, "Y"), ("A", 3, "G")], [("B", 0, "Y"), ("F", 2, "G")]),
    ([("WOT", 1, "Y"), ("A", 4, "G")], [("B", 1, "Y"), ("F", 3, "G")]),
    ([("WOT", 2, "Y"), ("A", 5, "G")], [("B", 2, "Y"), ("XT", 1, "G")]),
    ([("WOT", 3, "Y"), ("A", 6, "G")], [("B", 3, "Y"), ("CKV", 1, "G")]),
    ([("WOT", 4, "Y"), ("A", 7, "G")], [("SQUARES", 1, None), ("B", 4, "Y"), ("F", 4, "G")]),
    ([("WOT", 5, "Y"), ("F", 5, "G"), ("XSPLIT", 1, None)], [("B", 5, "Y"), ("F", 6, "G"), ("CNORM", 1, None)]),
    ([("WOT", 6, "Y"), ("KT", 1, "G")], [("F", 7, "T"), ("B", 6, "Y"), ("F", 8, "G")]),
    ([("WOT", 7, "Y"), ("F", 9, "G")], [("F", 10, "T"), ("B", 7, "Y"), ("F", 11, "G")]),
]
MIDDLE = [
    ([("OUTA", 0, None)], [("OUT", 0, "G")]),
    ([("OUT", 1, "Y")], [("XT", 1, "G")]),
    ([("CKV", 1, "Y")], [("X1T", 0, "G")]),
    ([("GU", 0, "Y")], [("SQUARES", 1, None), ("GU", 1, "G"), ("GU", 2, "Y")]),
    ([("GU", 3, "G")], [("CNORM", 1, None), ("GU", 4, "Y"), ("GU", 5, "G")]),
    ([("XSPLIT", 1, None), ("GU", 6, "Y")], [("GU", 7, "G")]),
    ([("KT", 1, "Y")], [("DN", 0, "G")]),
    ([("DN", 1, "Y")], []),
]
OF_NEXT = ("XT", "CKV", "SQUARES", "CNORM", "XSPLIT", "KT")


def in_last(s, ahead, behind):
    if s in (NP - 3, NP - 2):
        ahead, behind = ahead + behind, []
    if s >= NP - 2:
        ahead = [(kind, arg, {"G": "Y", "Y": "G"}[k]) for kind, arg, k in ahead]
    return tuple([e for e in events if e[0] not in OF_NEXT] for events in (ahead, behind))


LAST = [in_last(s, *events) for s, events in enumerate(MIDDLE)]
EPILOGUE = [("OUTA", 0, None), ("OUT", 0, "S"), ("OUT", 1, "R"), ("X1TILE", 0, "G"), ("X1TILE", 1, "Y"),
            ("GU", 0, "S"), ("GU", 1, "R"), ("GU", 2, "G"), ("GU", 3, "Y"), ("GU", 4, "S"), ("GU", 5, "R"),
            ("GU", 6, "G"), ("GU", 7, "Y"), ("DNA", 0, None), ("DNA", 1, None), ("DN", 0, "S"), ("DN", 1, "R")]
AHEAD = {"middle": (0, 0), "last": (0, 0), "epilogue": (NJ - 1, 2)}


def in_order(steps):
    return [e for ahead, behind in steps for e in ahead + behind]


DEFERRED = ("GU", "OUT", "DN")
LATE_SUM = 1
LOADS = [e[:2] for e in PROLOGUE + in_order(FIRST) if e[0] in "ABF"]


def layer(nc, x, wq, wkva, norm_w, wkvb, wo, cos, sin, w_gate, w_up, w_down, out):
    with ExitStack() as ctx:
        def sb(name, shape, dt=F32):
            return ctx.enter_context(nc.sbuf_tensor(name, shape, dt))

        def pb(name, shape):
            return ctx.enter_context(nc.psum_tensor(name, shape, F32))

        def sem(name):
            return ctx.enter_context(nc.semaphore(name))

        ident = sb("ident", [P, P])
        mask = sb("mask", [P, 2 * P])
        cosb = sb("cosb", [P, ROPE])
        sinb = sb("sinb", [P, ROPE])
        rot = sb("rot", [P, 2, ROPE])
        ropet = sb("ropet", [P, 2, ROPE])
        kfold = sb("kfold", [P, 2, ROPE])
        normw = sb("normw", [P, LORA])
        mhalf = sb("mhalf", [P, 2])
        stage = sb("stage", [P, SLOTS, SLOT])
        wkva_raw = sb("wkva_raw", [P, HID])
        wkvat = sb("wkvat", [P, NC, P])
        a_hi = sb("a_hi", [P, NC, NH, P], F32R)
        a_lo = sb("a_lo", [P, NC, NH, P], F32R)
        wot = sb("wot", [P, 2, HID])
        b_hi = sb("b_hi", [P, NP, HID], F32R)
        b_lo = sb("b_lo", [P, NP, HID], F32R)
        ff_hi = [sb(f"{n}_hi", [P, NC, FF], F32R) for n in ("gate", "up")] + [sb("down_hi", [P, NJ, HID], F32R)]
        ff_lo = [sb(f"{n}_lo", [P, NC, FF], F32R) for n in ("gate", "up")] + [sb("down_lo", [P, NJ, HID], F32R)]
        x_in = sb("x_in", [P, NT, HID])
        x_res = sb("x_res", [P, NT, HID])
        xt = sb("xt", [P, NC, S])
        xt_hi = sb("xt_hi", [P, NC, S], F32R)
        xt_lo = sb("xt_lo", [P, NC, S], F32R)
        ckv = sb("ckv", [P, NT, P])
        squares = sb("squares", [P, NT, LORA])
        ssq = sb("ssq", [P, NT])
        msq = sb("msq", [P, NT])
        rms = sb("rms", [P, NT])
        kt = sb("kt", [P, P])
        kt_hi = sb("kt_hi", [P, S], F32R)
        kt_lo = sb("kt_lo", [P, S], F32R)
        c_parts = sb("c_parts", [P, NT, 2, LORA], F32R)
        q0 = sb("q0", [P, 2, 2, P])
        q1_hi = sb("q1_hi", [P, 2, 2, P], F32R)
        q1_lo = sb("q1_lo", [P, 2, 2, P], F32R)
        prob = sb("prob", [P, 2, 3 * P])
        nmax = sb("nmax", [P, 2, 2])
        rowsum = sb("rowsum", [P, 2, 2])
        rrow = sb("rrow", [P, 2, 2])
        pt_hi = sb("pt_hi", [P, 2, 3 * P], F32R)
        pt_lo = sb("pt_lo", [P, 2, 3 * P], F32R)
        o_low = sb("o_low", [LORA, 2, S])
        o_sum = sb("o_sum", [P, 2, S])
        ot_hi = sb("ot_hi", [P, NP, S], F32R)
        ot_lo = sb("ot_lo", [P, NP, S], F32R)
        res = sb("res", [P, NT, HID])
        stats = sb("stats", [P, NT, 6])
        moments = sb("moments", [P, NT, 2])
        vareps = sb("vareps", [P, NT])
        rstd = sb("rstd", [P, NT])
        x1 = sb("x1", [P, NT, HID])
        x1t_hi = sb("x1t_hi", [P, NC, S], F32R)
        x1t_lo = sb("x1t_lo", [P, NC, S], F32R)
        act_g = sb("act_g", [P, 2, S])
        h_sum = sb("h_sum", [P, 2, S])
        h_hi = sb("h_hi", [P, NJ, S], F32R)
        h_lo = sb("h_lo", [P, NJ, S], F32R)
        y = sb("y", [P, NT, HID])

        q_ps = pb("q_ps", [P, 2, S])
        s_ps = [pb(f"s_ps{h}", [P, 512]) for h in range(2)]
        t_ps = [pb(f"t_ps{h}", [P, 512]) for h in range(2)]
        o_ps = pb("o_ps", [P, 2, S])
        bank = {"G": pb("g_ps", [P, 512]), "Y": pb("y_ps", [P, 512]), "S": s_ps[0], "R": s_ps[1], "T": t_ps[1]}

        x_in_loaded, x_res_loaded, rope_loaded = sem("x_in_loaded"), sem("x_res_loaded"), sem("rope_loaded")
        wkva_loaded, normw_loaded = sem("wkva_loaded"), sem("normw_loaded")
        slot_loaded = [sem(f"slot_loaded{i}") for i in range(SLOTS)]
        zeroed, ident_ready, mask_ready, rot_ready = (
            sem("zeroed"), sem("ident_ready"), sem("mask_ready"), sem("rot_ready"))
        rope_chain, rope_ready = sem("rope_chain"), sem("rope_ready")
        full = {k: sem(f"{k}_full") for k in bank}
        read = {(k, e): sem(f"{k}_read_by_{e}") for k in bank for e in ("act", "dve")}
        q_done, q_act_ready, q_lo_ready = sem("q_done"), sem("q_act_ready"), sem("q_lo_ready")
        s_done, max_ready, exp_ready, rrow_ready, prob_ready, t_done, pt_hi_ready, pt_lo_ready = (
            [sem(f"{n}{h}") for h in range(2)] for n in (
                "s_done", "max_ready", "exp_ready", "rrow_ready", "prob_ready", "t_done", "pt_hi_ready",
                "pt_lo_ready"))
        o_done, o_low_ready, o_sum_ready, ot_hi_ready, ot_ready = (
            sem("o_done"), sem("o_low_ready"), sem("o_sum_ready"), sem("ot_hi_ready"), sem("ot_ready"))
        ssq_ready, msq_ready, rms_ready, c_ready = (
            sem("ssq_ready"), sem("msq_ready"), sem("rms_ready"), sem("c_ready"))
        c_hi_ready, c_parts_ready, xt_hi_ready, xt_lo_ready = (
            sem("c_hi_ready"), sem("c_parts_ready"), sem("xt_hi_ready"), sem("xt_lo_ready"))
        out_half, x1_ready, y_ready, y_free = sem("out_half"), sem("x1_ready"), sem("y_ready"), sem("y_free")
        ln_chain, vareps_ready, rstd_ready = sem("ln_chain"), sem("vareps_ready"), sem("rstd_ready")
        tile_stats, tile_moments, tile_vareps, tile_rstd = (
            sem("tile_stats"), sem("tile_moments"), sem("tile_vareps"), sem("tile_rstd"))
        x1_tile_ready, y_tile_ready = sem("x1_tile_ready"), sem("y_tile_ready")
        dve_passed, pool_passed = sem("dve_passed"), sem("pool_passed")
        gated, h_hi_ready, h_ready = sem("gated"), sem("h_hi_ready"), sem("h_ready")

        def plan():
            now = {("full", k): 0 for k in bank} | {(k, e): 0 for k in bank for e in ("act", "dve")}
            last_use = dict.fromkeys(bank)
            uses = {}

            def add(part, events, slope):
                for kind, arg, k in events:
                    if k is None:
                        continue
                    before = [(e, now[k, e]) for e in ("act", "dve")
                              if last_use[k] and e in READERS[last_use[k]]]
                    now["full", k] += 1
                    for e in READERS[kind]:
                        now[k, e] += 1
                    last_use[k] = kind
                    uses[part, kind, arg] = (k, before, now["full", k], {e: now[k, e] for e in READERS[kind]},
                                             {i: slope(i) for i in now})

            add("prologue", PROLOGUE, lambda i: 0)
            add("first", in_order(FIRST), lambda i: 0)
            start = dict(now)
            add("middle", in_order(MIDDLE), lambda i: 0)
            growth = {i: now[i] - start[i] for i in now}
            for key, use in uses.items():
                if key[0] == "middle":
                    use[4].update(growth)
            for i in now:
                now[i] = start[i] + growth[i] * (NB - 2)
            add("last", in_order(LAST), lambda i: 0)
            add("epilogue", EPILOGUE, lambda i: 0)
            return uses

        uses = plan()

        class Use:

            def __init__(self, part, kind, arg, b):
                self.bank, self.before, self.filled, self.after, self.growth = uses[part, kind, arg]
                self.b = b
                self.ps = bank[self.bank]

            def value(self, count, i):
                grow = self.growth[i]
                return self.b * grow + (count - grow) if grow else count

            def wait_free(self, pe):
                for e, count in self.before:
                    pe.wait_ge(read[self.bank, e], self.value(count, (self.bank, e)))

            def wait_full(self, eng):
                eng.wait_ge(full[self.bank], self.value(self.filled, ("full", self.bank)))

            def wait_read(self, eng, e):
                eng.wait_ge(read[self.bank, e], self.value(self.after[e], (self.bank, e)))

            @property
            def is_full(self):
                return full[self.bank]

            def read_by(self, e):
                return read[self.bank, e]

        def done(b, s, more=0):
            return b * NP + (s + 1 + more)

        def hold(eng, semaphore, count, passed):
            eng.wait_ge(semaphore, count)
            eng.sem_inc(passed, 1)

        def after(b, s, n):
            return (b, s + n) if s + n < NP else (b + 1, s + n - NP)

        def run(eng, prologue, step, epilogue):
            def steps(of, left=None):
                for b, s, events, part in of:
                    ahead, behind = ([(kind, arg, part, b) for kind, arg, _ in some] for some in events)
                    leave = behind.pop() if behind and behind[-1][0] in DEFERRED else None
                    step(b, s, ahead, behind, leave, left, part)
                    left = leave
                return left

            def left_by_step_0(b):
                kind, arg, _ = MIDDLE[0][1][-1]
                return kind, arg, "middle", b

            prologue()
            steps([(0, s, FIRST[s], "first") for s in range(NP)] + [(1, 0, MIDDLE[0], "middle")])
            with eng.Fori(1, NB - 1) as b:
                steps([(b, s, MIDDLE[s], "middle") for s in range(1, NP)] + [(b + 1, 0, MIDDLE[0], "middle")],
                      left_by_step_0(b))
            left = steps([(NB - 1, s, LAST[s], "last") for s in range(1, NP)], left_by_step_0(NB - 1))
            assert left is None
            epilogue([(kind, arg, "epilogue", NB) for kind, arg, _ in EPILOGUE])

        def halves(ahead):
            early = [e for e in ahead if e[0] == "GU"][:1]
            return early, [e for e in ahead if e not in early]

        def with_last(behind, leave):
            return behind + [leave] * bool(leave)

        def follows(b, s, n):
            return not (isinstance(b, int) and b * NP + s + n >= NB * NP)

        a_of = {n: i for i, n in enumerate(LOADS)}

        def slot_of(kind, arg):
            return stage[:, a_of[kind, arg] % SLOTS, :], slot_loaded[a_of[kind, arg] % SLOTS]

        N_DMAS = {"A": 4, "B": 2, "F": 1}

        def slot_count(kind, arg):
            n = a_of[kind, arg]
            return 16 * sum(N_DMAS[k] for k, _ in LOADS[n % SLOTS:n + 1:SLOTS])

        block = ctx.enter_context(nc.Block())

        @block.sync
        def _(sp):
            def load_x(b):
                sp.dma_start(x_in[:, :, :], x[b].rearrange("(t p) c -> p t c", p=P)).then_inc(x_in_loaded, 16)

            def load_res(b):
                sp.dma_start(x_res[:, :, :], x[b].rearrange("(t p) c -> p t c", p=P)).then_inc(x_res_loaded, 16)

            def store_y(b):
                sp.wait_ge(y_ready, b + 1)
                sp.dma_start(out[b].rearrange("(t p) c -> p t c", p=P), y[:, :, :]).then_inc(y_free, 16)

            def load_weights(n):
                kind, i = LOADS[n]
                to, loaded = slot_of(kind, i)
                if n >= SLOTS:
                    k, j = LOADS[n - SLOTS]
                    part = "prologue" if ("prologue", k, j) in uses else "first"
                    Use(part, k, j, 0).wait_full(sp)
                if kind == "A":
                    heads = wq.rearrange("(h r) c -> r h c", r=DQ)[:, 2 * i:2 * i + 2, :]
                    kv = wkvb.rearrange("(h r) c -> r h c", r=NOPE + DV)[0:NOPE, 2 * i:2 * i + 2, :]
                    sp.dma_start(to[:, 0:512].rearrange("p (h c) -> p h c", h=2), heads[0:NOPE]).then_inc(loaded, 16)
                    sp.dma_start(to[:, 512:640].rearrange("p (h c) -> p h c", h=2), kv).then_inc(loaded, 16)
                    for h in range(2):
                        sp.dma_start(to[h * ROPE:(h + 1) * ROPE, 640:896], heads[NOPE:DQ, h, :]).then_inc(loaded, 16)
                elif kind == "B":
                    kv = wkvb.rearrange("(h r) c -> r h c", r=NOPE + DV)[NOPE:NOPE + DV, 2 * i:2 * i + 2, :]
                    cols = wo[:, 2 * i * DV:2 * (i + 1) * DV].rearrange("(o p) c -> p o c", p=P)
                    sp.dma_start(to[:, 0:512].rearrange("p (o c) -> p o c", o=2), cols).then_inc(loaded, 16)
                    sp.dma_start(to[:, 512:640].rearrange("p (h c) -> p h c", h=2), kv).then_inc(loaded, 16)
                else:
                    which, jj = divmod(i, 4)
                    if which < 2:
                        w = (w_gate, w_up)[which].rearrange("(j p) c -> p j c", p=P)[:, 2 * jj:2 * jj + 2, :]
                    else:
                        w = w_down[:, 2 * jj * P:2 * (jj + 1) * P].rearrange("(o p) c -> p o c", p=P)
                    sp.dma_start(to[:, 0:512].rearrange("p (j c) -> p j c", j=2), w).then_inc(loaded, 16)

            for to, of in ((cosb, cos), (sinb, sin)):
                sp.dma_start(to[:, :], of.partition_broadcast(P)).then_inc(rope_loaded, 16)
            sp.dma_start(wkva_raw[:, :], wkva).then_inc(wkva_loaded, 16)
            load_x(0)
            for n in range(len(LOADS)):
                load_weights(n)
                if n == 0:
                    sp.dma_start(normw[:, :], norm_w.rearrange("(a n) -> a n", a=1).partition_broadcast(P))\
                      .then_inc(normw_loaded, 16)
                if n == 1:
                    Use("prologue", "XT", 0, 0).wait_full(sp)
                    load_x(1)
                if n == 5:
                    load_res(0)
            Use("first", "XT", 1, 0).wait_full(sp)
            load_x(2)
            with sp.Fori(1, NB - 2) as b:
                Use("middle", "OUT", 1, b).wait_read(sp, "dve")
                load_res(b)
                Use("middle", "XT", 1, b).wait_full(sp)
                load_x(b + 2)
                store_y(b - 1)
            Use("middle", "OUT", 1, NB - 2).wait_read(sp, "dve")
            load_res(NB - 2)
            store_y(NB - 3)
            Use("last", "OUT", 1, NB - 1).wait_read(sp, "dve")
            load_res(NB - 1)
            store_y(NB - 2)
            for t in range(NT):
                sp.wait_ge(y_tile_ready, t + 1)
                sp.dma_start(out[NB - 1, t * P:(t + 1) * P, :], y[:, t, :]).then_inc(y_free, 16)
            sp.wait_ge(y_free, 16 * (NB + NT))

        @block.tensor
        def _(pe):
            def three(ps, w_hi, w_lo, m_hi, m_lo, start, stop):
                nc.tensor.matmul(ps, w_hi, m_hi, start=start, stop=False)
                nc.tensor.matmul(ps, w_hi, m_lo, start=False, stop=False)
                return nc.tensor.matmul(ps, w_lo, m_hi, start=False, stop=stop)

            def transposes(b, s, wait_bank):
                for h in range(2):
                    if h == 1:
                        wait_bank()
                    pe.wait_ge(prob_ready[h], done(b, s))
                    for i in range(3):
                        last = nc.tensor.transpose(t_ps[h][:, i * P:(i + 1) * P], prob[:, h, i * P:(i + 1) * P],
                                                   ident[:, :])
                    last.then_inc(t_done[h], 1)

            def queries(b, s):
                if s == 0:
                    pe.wait_ge(xt_hi_ready, b + 1)
                    pe.wait_ge(xt_lo_ready, b + 1)
                if isinstance(b, int) and b == 0:
                    part = "prologue" if s < 3 else "first"
                    Use(part, "A", s, 0).wait_read(pe, "dve")
                for h in range(2):
                    n = 2 * s + h
                    for c in range(NC):
                        last = three(q_ps[:, h, :], a_hi[:, c, n, :], a_lo[:, c, n, :], xt_hi[:, c, :],
                                     xt_lo[:, c, :], c == 0, c == NC - 1)
                last.then_inc(q_done, 1)

            def scores(b, s):
                pe.wait_ge(q_lo_ready, done(b, s))
                i = s % 2
                for h in range(2):
                    nc.tensor.matmul(s_ps[h][:, 0:P], q0[:, i, h, :], kt[:, :], start=True, stop=True)
                    three(s_ps[h][:, P:3 * P], q1_hi[:, i, h, :], q1_lo[:, i, h, :], kt_hi[:, :], kt_lo[:, :],
                          True, True).then_inc(s_done[h], 1)

            def values(b, s):
                for h in range(2):
                    pe.wait_ge(pt_lo_ready[h], done(b, s))
                if s == 0:
                    pe.wait_ge(c_parts_ready, b + 1)
                if not (isinstance(b, int) and b == 0 and s == 0):
                    pe.wait_ge(o_sum_ready, done(b, s, -1))
                for k in range(NT):
                    cols = slice(0, S) if k == 0 else slice(S, S + P)
                    for pt in (pt_hi, pt_lo):
                        last = nc.tensor.matmul(o_ps[:, :, k * P:S], c_parts[:, k, :, :], pt[:, :, cols],
                                                start=(k == 0 and pt is pt_hi), stop=(k == 1 and pt is pt_lo))
                last.then_inc(o_done, 1)

            def project(b, ps, t, pairs):
                cols = slice(t * P, (t + 1) * P)
                for p in pairs:
                    if t == 0 and p >= NP // 2:
                        pe.wait_ge(ot_ready, done(b - 1, p))
                    last = three(ps[:, 0:HID], ot_hi[:, p, cols], ot_lo[:, p, cols], b_hi[:, p, :],
                                 b_lo[:, p, :], p == 0, p == NP - 1)
                return last

            def down(b, ps, t, chunks):
                cols = slice(t * P, (t + 1) * P)
                for j in chunks:
                    if t == 0:
                        pe.wait_ge(h_ready, (b - 1) * NJ + (j + 1))
                    last = three(ps[:, 0:HID], h_hi[:, j, cols], h_lo[:, j, cols], ff_hi[2][:, j, :],
                                 ff_lo[2][:, j, :], j == 0, j == NJ - 1)
                return last

            def event(kind, arg, part, b):
                if kind in ("SQUARES", "CNORM", "XSPLIT"):
                    return
                if kind == "OUTA":
                    pe.wait_ge(ot_ready, done(b - 1, NP // 2 - 1))
                    for t in range(2):
                        Use(part, "OUT", t, b).wait_free(pe)
                        last = project(b, Use(part, "OUT", t, b).ps, t, range(NP // 2))
                    last.then_inc(out_half, 1)
                    return
                if kind == "DNA":
                    use = Use(part, "DN", arg, b)
                    use.wait_free(pe)
                    down(b, use.ps, arg, range(AHEAD[part][arg]))
                    return
                use = Use(part, kind, arg, b)
                ps = use.ps
                if kind != "OUT" and (kind != "DN" or AHEAD[part][arg] == 0):
                    use.wait_free(pe)
                if kind == "XT":
                    nb = b + arg
                    pe.wait_ge(x_in_loaded, (nb + 1) * 16)
                    if part == "prologue":
                        pe.wait_ge(ident_ready, 1)
                    for c in range(NC):
                        for t in range(NT):
                            last = nc.tensor.transpose(ps[:, c * S + t * P:c * S + (t + 1) * P],
                                                       x_in[:, t, c * P:(c + 1) * P], ident[:, :])
                elif kind == "WKVA":
                    pe.wait_ge(wkva_loaded, 16)
                    pe.wait_ge(rope_ready, 2)
                    for c in range(NC):
                        last = nc.tensor.matmul(ps[:, c * P:(c + 1) * P], wkva_raw[:, c * P:(c + 1) * P],
                                                kfold[:, :, :], start=True, stop=True)
                elif kind == "CKV":
                    Use(part, "XT", arg, b).wait_read(pe, "act")
                    if part == "prologue":
                        Use(part, "WKVA", 0, 0).wait_read(pe, "dve")
                    for t in range(NT):
                        for c in range(NC):
                            last = nc.tensor.matmul(ps[:, t * P:(t + 1) * P], xt[:, c, t * P:(t + 1) * P],
                                                    wkvat[:, c, :], start=(c == 0), stop=(c == NC - 1))
                elif kind == "KT":
                    pe.wait_ge(c_ready, b + arg + 1)
                    for t in range(NT):
                        last = nc.tensor.transpose(ps[:, t * P:(t + 1) * P], ckv[:, t, :], ident[:, :])
                elif kind == "A":
                    w, loaded = slot_of("A", arg)
                    pe.wait_ge(loaded, slot_count("A", arg))
                    for c in range(NC):
                        for h in range(2):
                            nc.tensor.matmul(ps[:, c * S + h * LORA:c * S + h * LORA + P],
                                             w[:, h * HID + c * P:h * HID + (c + 1) * P],
                                             w[:, 512 + h * LORA:512 + h * LORA + P], start=True, stop=True)
                        last = nc.tensor.matmul(ps[:, c * S + P:(c + 1) * S], w[:, 640 + c * P:640 + (c + 1) * P],
                                                ropet[:, :, :], start=True, stop=True)
                elif kind == "WOT":
                    w, loaded = slot_of("B", arg)
                    pe.wait_ge(loaded, slot_count("B", arg))
                    for h in range(2):
                        for o in range(NC):
                            last = nc.tensor.transpose(ps[:, h * HID + o * P:h * HID + (o + 1) * P],
                                                       w[:, o * 256 + h * P:o * 256 + (h + 1) * P], ident[:, :])
                elif kind == "B":
                    w, _ = slot_of("B", arg)
                    Use(part, "WOT", arg, 0).wait_read(pe, "dve")
                    for h in range(2):
                        last = nc.tensor.matmul(ps[:, h * HID:(h + 1) * HID], w[:, 512:640], wot[:, h, :],
                                                start=True, stop=True)
                elif kind == "F":
                    w, loaded = slot_of("F", arg)
                    pe.wait_ge(loaded, slot_count("F", arg))
                    for j in range(2):
                        for c in range(2):
                            at = c * 256 + j * P if arg < 8 else j * 256 + c * P
                            src = j * 256 + c * P if arg < 8 else c * 256 + j * P
                            last = nc.tensor.transpose(ps[:, at:at + P], w[:, src:src + P], ident[:, :])
                elif kind == "X1T":
                    pe.wait_ge(x1_ready, b)
                    for c in range(NC):
                        for t in range(NT):
                            last = nc.tensor.transpose(ps[:, c * S + t * P:c * S + (t + 1) * P],
                                                       x1[:, t, c * P:(c + 1) * P], ident[:, :])
                elif kind == "X1TILE":
                    pe.wait_ge(x1_tile_ready, arg + 1)
                    for c in range(NC):
                        last = nc.tensor.transpose(ps[:, c * P:(c + 1) * P], x1[:, arg, c * P:(c + 1) * P],
                                                   ident[:, :])
                elif kind == "GU":
                    if arg == 0:
                        if part == "epilogue":
                            Use(part, "X1TILE", NT - 1, b).wait_read(pe, "dve")
                        else:
                            Use(part, "X1T", 0, b).wait_read(pe, "dve")
                    cols = slice(arg * P, (arg + 1) * P)
                    for g in range(2):
                        for c in range(NC):
                            last = three(ps[:, g * S:(g + 1) * S], ff_hi[g][:, c, cols], ff_lo[g][:, c, cols],
                                         x1t_hi[:, c, :], x1t_lo[:, c, :], c == 0, c == NC - 1)
                elif kind == "OUT":
                    last = project(b, ps, arg, range(NP // 2, NP))
                elif kind == "DN":
                    last = down(b, ps, arg, range(AHEAD[part][arg], NJ))
                last.then_inc(use.is_full, 1)

            def keep_busy(n):
                for _ in range(n):
                    nc.tensor.transpose(t_ps[0][:, 0:P], ident[:, :], ident[:, :])

            def prologue():
                pe.wait_ge(ident_ready, 1)
                keep_busy(9)
                event("WKVA", 0, "prologue", 0)
                event("XT", 0, "prologue", 0)
                keep_busy(4)
                for kind, arg in (("CKV", 0), ("A", 0), ("A", 1), ("KT", 0)):
                    event(kind, arg, "prologue", 0)
                queries(0, 0)
                event("A", 2, "prologue", 0)
                Use("prologue", "KT", 0, 0).wait_read(pe, "dve")
                scores(0, 0)
                queries(0, 1)
                for j in range(2):
                    event("F", j, "prologue", 0)

            def step(b, s, ahead, behind, leave, left, part):
                def wait_bank():
                    if (part, s) != ("first", 0) and (part == "first" or (s == 0 and isinstance(b, int))):
                        for kind, arg, k in FIRST[s - 1][1]:
                            if k == "T":
                                Use("first", kind, arg, 0).wait_read(pe, READERS[kind][-1])

                transposes(b, s, wait_bank)
                if follows(b, s, 1):
                    if s == NP - 1:
                        Use(part, "KT", 1, b).wait_read(pe, "dve")
                    scores(*after(b, s, 1))
                if follows(b, s, 2):
                    queries(*after(b, s, 2))
                for e in ahead:
                    event(*e)
                values(b, s)
                for e in with_last(behind, leave):
                    event(*e)

            def epilogue(events):
                for e in events:
                    event(*e)
                    keep_busy({("OUT", NT - 1): 16, ("X1TILE", 0): 4, ("X1TILE", NT - 1): 8}.get(e[:2], 0))

            run(pe, prologue, step, epilogue)

        @block.scalar
        def _(act):
            def copy(to, of):
                return nc.scalar.activation(to, of, ACT.Copy)

            def pt_high(b, s, h):
                act.wait_ge(t_done[h], done(b, s))
                copy(pt_hi[:, h, :], t_ps[h][:, 0:3 * P]).then_inc(pt_hi_ready[h], 1)

            def q_parts(b, s):
                act.wait_ge(q_done, done(b, s))
                copy(q0[:, s % 2, :, :], q_ps[:, :, 0:P])
                copy(q1_hi[:, s % 2, :, :], q_ps[:, :, P:S]).then_inc(q_act_ready, 1)

            def exps(b, s, h):
                act.wait_ge(max_ready[h], done(b, s))
                for t, cols in ((0, slice(0, P)), (1, slice(P, 3 * P))):
                    last = nc.scalar.activation(prob[:, h, cols], prob[:, h, cols], ACT.Exp,
                                                bias=nmax[:, h, t:t + 1], scale=-1.0,
                                                accum_out=rowsum[:, h, t:t + 1])
                last.then_inc(exp_ready[h], 1)

            def o_low_half(b, s):
                act.wait_ge(o_done, done(b, s))
                copy(o_low[:, :, :], o_ps[LORA:P, :, :]).then_inc(o_low_ready, 1)

            def event(kind, arg, part, b):
                if kind == "XSPLIT":
                    if part != "prologue":
                        act.wait_ge(q_done, done(b, NP - 1))
                    copy(xt_hi[:, :, :], xt[:, :, :]).then_inc(xt_hi_ready, 1)
                    return
                if kind == "SQUARES":
                    Use(part, "CKV", arg, b).wait_read(act, "act")
                    for t in range(NT):
                        last = nc.scalar.activation(squares[:, t, :], ckv[:, t, 0:LORA], ACT.Square,
                                                    accum_out=ssq[:, t:t + 1])
                    last.then_inc(ssq_ready, 1)
                    return
                if kind not in READERS or "act" not in READERS[kind]:
                    return
                use = Use(part, kind, arg, b)
                ps = use.ps
                use.wait_full(act)
                if kind == "XT":
                    last = copy(xt[:, :, :], ps[:, :])
                elif kind == "CKV":
                    last = copy(ckv[:, :, :], ps[:, 0:NT * P])
                elif kind == "KT":
                    copy(kt[:, :], ps[:, 0:P])
                    last = copy(kt_hi[:, :], ps[:, 0:S])
                elif kind == "A":
                    for c in range(NC):
                        last = copy(a_hi[:, c, 2 * arg:2 * arg + 2, :].rearrange("p h (k d) -> p k h d", k=2),
                                    ps[:, c * S:(c + 1) * S].rearrange("p (k h d) -> p k h d", k=2, h=2))
                elif kind == "B":
                    for h in range(2):
                        rows = slice(h * LORA, (h + 1) * LORA)
                        last = copy(b_hi[rows, arg, :], ps[rows, h * HID:(h + 1) * HID])
                elif kind == "F":
                    which, jj = divmod(arg, 4)
                    if which < 2:
                        last = copy(ff_hi[which][:, :, jj * 256:(jj + 1) * 256],
                                    ps[:, :].rearrange("p (c j) -> p c j", c=2))
                    else:
                        last = copy(ff_hi[2][:, 2 * jj:2 * jj + 2, :], ps[:, :])
                elif kind == "X1T":
                    last = copy(x1t_hi[:, :, :], ps[:, :])
                elif kind == "X1TILE":
                    last = copy(x1t_hi[:, :, arg * P:(arg + 1) * P], ps[:, 0:NC * P])
                elif kind == "GU":
                    if arg >= 2:
                        Use(part, "GU", arg - 2, b).wait_read(act, "dve")
                    last = nc.scalar.activation(act_g[:, arg % 2, :], ps[:, 0:S], ACT.Tanh, scale=0.5)
                last.then_inc(use.read_by("act"), 1)

            def prologue():
                event("XT", 0, "prologue", 0)
                Use("prologue", "XT", 0, 0).wait_read(act, "act")
                event("XSPLIT", 0, "prologue", 0)
                for kind, arg in (("CKV", 0), ("SQUARES", 0), ("A", 0), ("A", 1), ("KT", 0)):
                    event(kind, arg, "prologue", 0)
                q_parts(0, 0)
                event("A", 2, "prologue", 0)
                for h in range(2):
                    exps(0, 0, h)
                q_parts(0, 1)
                for j in range(2):
                    event("F", j, "prologue", 0)

            def step(b, s, ahead, behind, leave, left, part):
                for h in range(2):
                    pt_high(b, s, h)
                if s == LATE_SUM + 1 and part == "middle":
                    event("XT", 1, part, b)
                if follows(b, s, 1):
                    for h in range(2):
                        exps(*after(b, s, 1), h)
                early, late = halves(ahead)
                for e in early:
                    event(*e)
                if follows(b, s, 2):
                    q_parts(*after(b, s, 2))
                for e in late:
                    event(*e)
                o_low_half(b, s)
                for e in with_last(behind, leave):
                    if e[:3] != ("XT", 1, "middle"):
                        event(*e)

            def epilogue(events):
                for e in events:
                    event(*e)

            run(act, prologue, step, epilogue)

        @block.vector
        def _(dve):
            tt, stt = nc.vector.tensor_tensor, nc.vector.scalar_tensor_tensor

            def low(to, of, high):
                return tt(to, of, high.bitcast(F32), ALU.subtract)

            def pt_low(b, s, h):
                dve.wait_ge(pt_hi_ready[h], done(b, s))
                low(pt_lo[:, h, :], t_ps[h][:, 0:3 * P], pt_hi[:, h, :]).then_inc(pt_lo_ready[h], 1)

            def maxima(b, s, h):
                hold(dve, s_done[h], done(b, s), dve_passed)
                for t, cols in ((0, slice(0, P)), (1, slice(P, 3 * P))):
                    last = nc.vector.tensor_tensor_reduce(
                        out=prob[:, h, cols], in0=s_ps[h][:, cols], in1=mask[:, (1 - t) * P:2 * P], scale=-SCALE,
                        scalar=TOP, op0=ALU.add, op1=ALU.min, accum_out=nmax[:, h, t:t + 1])
                last.then_inc(max_ready[h], 1)

            def row_reciprocals(b, s, h):
                dve.wait_ge(exp_ready[h], done(b, s))
                nc.vector.reciprocal(rrow[:, h, :], rowsum[:, h, :]).then_inc(rrow_ready[h], 1)

            def q_low(b, s):
                dve.wait_ge(q_act_ready, done(b, s))
                low(q1_lo[:, s % 2, :, :], q_ps[:, :, P:S], q1_hi[:, s % 2, :, :]).then_inc(q_lo_ready, 1)

            def o_add(b, s):
                dve.wait_ge(o_low_ready, done(b, s))
                if not (isinstance(b, int) and b == 0 and s < 2):
                    dve.wait_ge(ot_ready, done(b, s, -2))
                for h in range(2):
                    last = tt(o_sum[h * LORA:(h + 1) * LORA, s % 2, :], o_ps[0:LORA, h, :], o_low[:, h, :], ALU.add)
                last.then_inc(o_sum_ready, 1)

            def ln_sum(n, residual, t, use):
                use.wait_full(dve)
                tt(res[:, t, :], use.ps[:, 0:HID], residual[:, t, :], ALU.add).then_inc(use.read_by("dve"), 1)
                use.wait_read(dve, "dve")
                last = nc.vector.bn_stats(stats[:, t, :], res[:, t, :])
                if t < NT - 1:
                    return
                last.then_inc(ln_chain, 1)
                hold(dve, ln_chain, n * 2 + 1, dve_passed)
                for t in range(NT):
                    last = nc.vector.bn_aggr(moments[:, t, :], stats[:, t, :])
                last.then_inc(ln_chain, 1)
                dve.wait_ge(ln_chain, n * 2 + 2)
                nc.vector.tensor_scalar(vareps[:, :], moments[:, :, 1], LN_EPS, None, ALU.add).then_inc(vareps_ready, 1)

            def norm_by_tile(i, residual, to, ready, uses_):
                for t, use in enumerate(uses_):
                    n = i * NT + t + 1
                    use.wait_full(dve)
                    tt(res[:, t, :], use.ps[:, 0:HID], residual[:, t, :], ALU.add).then_inc(use.read_by("dve"), 1)
                    use.wait_read(dve, "dve")
                    nc.vector.bn_stats(stats[:, t, :], res[:, t, :]).then_inc(tile_stats, 1)
                    hold(dve, tile_stats, n, dve_passed)
                    nc.vector.bn_aggr(moments[:, t, :], stats[:, t, :]).then_inc(tile_moments, 1)
                    dve.wait_ge(tile_moments, n)
                    nc.vector.tensor_scalar(vareps[:, t:t + 1], moments[:, t, 1:2], LN_EPS, None, ALU.add)\
                        .then_inc(tile_vareps, 1)
                for t in range(NT):
                    dve.wait_ge(tile_rstd, i * NT + t + 1)
                    nc.vector.tensor_scalar(to[:, t, :], res[:, t, :], moments[:, t, 0:1], rstd[:, t:t + 1],
                                            ALU.subtract, ALU.mult).then_inc(ready, 1)

            def ln_scale(n, to, ready):
                dve.wait_ge(rstd_ready, n + 1)
                for t in range(NT):
                    last = nc.vector.tensor_scalar(to[:, t, :], res[:, t, :], moments[:, t, 0:1], rstd[:, t:t + 1],
                                                   ALU.subtract, ALU.mult)
                last.then_inc(ready, 1)

            def ln2_scale(f):
                dve.wait_ge(y_free, f * 16 + 16)
                ln_scale(f * 2 + 1, y, y_ready)

            def event(kind, arg, part, b):
                if kind == "XSPLIT":
                    dve.wait_ge(xt_hi_ready, b + arg + 1)
                    low(xt_lo[:, :, :], xt[:, :, :], xt_hi[:, :, :]).then_inc(xt_lo_ready, 1)
                elif kind == "CNORM":
                    if part == "prologue":
                        dve.wait_ge(normw_loaded, 16)
                    dve.wait_ge(rms_ready, b + arg + 1)
                    for t in range(NT):
                        last = stt(ckv[:, t, 0:LORA], ckv[:, t, 0:LORA], rms[:, t:t + 1], normw[:, :], ALU.mult,
                                   ALU.mult)
                    last.then_inc(c_ready, 1)
                elif kind == "SQUARES":
                    dve.wait_ge(ssq_ready, b + arg + 1)
                    nc.vector.tensor_scalar(msq[:, :], ssq[:, :], 1.0 / LORA, RMS_EPS, ALU.mult, ALU.add)\
                      .then_inc(msq_ready, 1)
                elif kind == "OUT":
                    if arg == 0:
                        dve.wait_ge(x_res_loaded, b * 16)
                    ln_sum((b - 1) * 2, x_res, arg, Use(part, kind, arg, b))
                elif kind == "DN":
                    if arg == 0:
                        dve.wait_ge(x1_ready, b)
                    ln_sum((b - 1) * 2 + 1, x1, arg, Use(part, kind, arg, b))
                if kind not in ("WKVA", "WOT", "A", "KT", "B", "F", "X1T", "X1TILE", "GU"):
                    return
                use = Use(part, kind, arg, b)
                ps = use.ps
                if kind == "WKVA":
                    use.wait_full(dve)
                    last = nc.vector.tensor_copy(wkvat[:, :, :], ps[:, 0:NC * P])
                elif kind == "WOT":
                    use.wait_full(dve)
                    last = nc.vector.tensor_copy(wot[:, :, :], ps[:, :])
                else:
                    use.wait_read(dve, "act")
                if kind == "KT":
                    last = low(kt_lo[:, :], ps[:, 0:S], kt_hi[:, :])
                elif kind == "A":
                    for c in range(NC):
                        last = low(a_lo[:, c, 2 * arg:2 * arg + 2, :].rearrange("p h (k d) -> p k h d", k=2),
                                   ps[:, c * S:(c + 1) * S].rearrange("p (k h d) -> p k h d", k=2, h=2),
                                   a_hi[:, c, 2 * arg:2 * arg + 2, :].rearrange("p h (k d) -> p k h d", k=2))
                elif kind == "B":
                    for h in range(2):
                        rows = slice(h * LORA, (h + 1) * LORA)
                        last = low(b_lo[rows, arg, :], ps[rows, h * HID:(h + 1) * HID], b_hi[rows, arg, :])
                elif kind == "F":
                    which, jj = divmod(arg, 4)
                    if which < 2:
                        cols = slice(jj * 256, (jj + 1) * 256)
                        last = low(ff_lo[which][:, :, cols], ps[:, :].rearrange("p (c j) -> p c j", c=2),
                                   ff_hi[which][:, :, cols])
                    else:
                        last = low(ff_lo[2][:, 2 * jj:2 * jj + 2, :], ps[:, :].rearrange("p (j c) -> p j c", j=2),
                                   ff_hi[2][:, 2 * jj:2 * jj + 2, :])
                elif kind == "X1T":
                    last = low(x1t_lo[:, :, :], ps[:, :].rearrange("p (c s) -> p c s", c=NC), x1t_hi[:, :, :])
                elif kind == "X1TILE":
                    cols = slice(arg * P, (arg + 1) * P)
                    last = low(x1t_lo[:, :, cols], ps[:, 0:NC * P].rearrange("p (c s) -> p c s", c=NC),
                               x1t_hi[:, :, cols])
                elif kind == "GU":
                    i = arg % 2
                    stt(act_g[:, i, :], act_g[:, i, :], 1.0, ps[:, 0:S], ALU.add, ALU.mult).then_inc(gated, 1)
                    dve.wait_ge(gated, (b - 1) * NJ + (arg + 1))
                    if arg >= 2:
                        dve.wait_ge(h_ready, (b - 1) * NJ + (arg - 1))
                    last = stt(h_sum[:, i, :], act_g[:, i, :], 0.5, ps[:, S:2 * S], ALU.mult, ALU.mult)
                last.then_inc(use.read_by("dve"), 1)

            def prologue():
                dve.wait_ge(rope_loaded, 16 * 2)
                dve.wait_ge(ident_ready, 1)
                dve.wait_ge(rot_ready, 2)
                for k in range(2):
                    tt(rot[:, k, :], rot[:, k, :], sinb[:, :], ALU.mult)
                    last = tt(ropet[:, k, :], cosb[:, :], ident[:, k * ROPE:(k + 1) * ROPE], ALU.mult)
                last.then_inc(rope_chain, 1)
                dve.wait_ge(rope_chain, 1)
                tt(ropet[:, :, :], ropet[:, :, :], rot[:, :, :], ALU.add).then_inc(rope_ready, 1)
                nc.vector.tensor_copy(kfold[:, 0, :], ident[:, 0:LORA])
                dve.wait_ge(rope_ready, 1)
                nc.vector.tensor_copy(kfold[:, 1, :], ropet[:, 1, :]).then_inc(rope_ready, 1)
                event("WKVA", 0, "prologue", 0)
                for kind, arg in (("XSPLIT", 0), ("SQUARES", 0), ("CNORM", 0), ("A", 0), ("A", 1), ("KT", 0)):
                    event(kind, arg, "prologue", 0)
                q_low(0, 0)
                dve.wait_ge(mask_ready, 1)
                for h in range(2):
                    maxima(0, 0, h)
                event("A", 2, "prologue", 0)
                for h in range(2):
                    row_reciprocals(0, 0, h)
                q_low(0, 1)
                for j in range(2):
                    event("F", j, "prologue", 0)

            def step(b, s, ahead, behind, leave, left, part):
                pt_low(b, s, 0)
                if follows(b, s, 1):
                    for h in range(2):
                        maxima(*after(b, s, 1), h)
                if s == LATE_SUM + 1 and part != "first":
                    o_add(b, LATE_SUM)
                pt_low(b, s, 1)
                if follows(b, s, 1):
                    row_reciprocals(*after(b, s, 1), 0)
                if left:
                    event(*left)
                if s == 0 and not isinstance(b, int):
                    ln2_scale(b - 2)
                if s == 2 and part != "first":
                    ln_scale((b - 1) * 2, x1, x1_ready)
                early, late = halves(ahead)
                for e in late:
                    if e[0] == "WOT":
                        event(*e)
                if follows(b, s, 1):
                    row_reciprocals(*after(b, s, 1), 1)
                for e in early:
                    event(*e)
                if follows(b, s, 2):
                    q_low(*after(b, s, 2))
                for e in late:
                    if e[0] != "WOT":
                        event(*e)
                if s != LATE_SUM or part == "first":
                    o_add(b, s)
                for e in behind:
                    event(*e)

            def epilogue(events):
                ln2_scale(NB - 2)
                dve.wait_ge(x_res_loaded, NB * 16)
                dve.wait_ge(y_ready, NB - 1)
                norm_by_tile(0, x_res, x1, x1_tile_ready, [Use("epilogue", "OUT", t, NB) for t in range(NT)])
                for e in events:
                    if e[0] in ("X1TILE", "GU"):
                        event(*e)
                dve.wait_ge(x1_tile_ready, NT)
                dve.wait_ge(y_free, NB * 16)
                norm_by_tile(1, x1, y, y_tile_ready, [Use("epilogue", "DN", t, NB) for t in range(NT)])

            run(dve, prologue, step, epilogue)

        @block.gpsimd
        def _(pool):
            def keep(to, of):
                return nc.gpsimd.tensor_scalar(to, of, 1.0, 1.0, ALU.mult, ALU.mult)

            def normalise(b, s, h):
                hold(pool, rrow_ready[h], done(b, s), pool_passed)
                for t, cols in ((0, slice(0, P)), (1, slice(P, 3 * P))):
                    last = nc.gpsimd.tensor_scalar(prob[:, h, cols], prob[:, h, cols], rrow[:, h, t:t + 1], 1.0,
                                                   ALU.mult, ALU.mult)
                last.then_inc(prob_ready[h], 1)

            def o_split(b, s):
                pool.wait_ge(o_sum_ready, done(b, s))
                if not (isinstance(b, int) and b == 0):
                    if s == 0:
                        pool.wait_ge(out_half, b)
                    if s == NP // 2:
                        Use("middle", "OUT", 1, b).wait_full(pool)
                pool.sem_inc(pool_passed, 1)
                keep(ot_hi[:, s, :], o_sum[:, s % 2, :]).then_inc(ot_hi_ready, 1)
                pool.wait_ge(ot_hi_ready, done(b, s))
                nc.gpsimd.tensor_tensor(ot_lo[:, s, :], o_sum[:, s % 2, :], ot_hi[:, s, :].bitcast(F32), ALU.subtract)\
                    .then_inc(ot_ready, 1)

            def c_split(nb):
                pool.wait_ge(c_ready, nb + 1)
                if not isinstance(nb, int) or nb > 0:
                    pool.wait_ge(o_done, nb * NP)
                pool.sem_inc(pool_passed, 1)
                keep(c_parts[:, :, 0, :], ckv[:, :, 0:LORA]).then_inc(c_hi_ready, 1)
                pool.wait_ge(c_hi_ready, nb + 1)
                nc.gpsimd.tensor_tensor(c_parts[:, :, 1, :], ckv[:, :, 0:LORA], c_parts[:, :, 0, :].bitcast(F32),
                                        ALU.subtract).then_inc(c_parts_ready, 1)

            def event(kind, arg, part, b):
                if kind == "SQUARES":
                    pool.wait_ge(msq_ready, b + arg + 1)
                    nc.gpsimd.tensor_tensor(rms[:, :], msq[:, :], mhalf[:, :], ALU.pow).then_inc(rms_ready, 1)
                elif kind in ("OUT", "DN") and arg == NT - 1:
                    n = (b - 1) * 2 + (kind == "DN")
                    pool.wait_ge(vareps_ready, n + 1)
                    nc.gpsimd.tensor_tensor(rstd[:, :], vareps[:, :], mhalf[:, :], ALU.pow).then_inc(rstd_ready, 1)
                elif kind == "GU":
                    Use(part, kind, arg, b).wait_read(pool, "dve")
                    pool.sem_inc(pool_passed, 1)
                    keep(h_hi[:, arg, :], h_sum[:, arg % 2, :]).then_inc(h_hi_ready, 1)
                    pool.wait_ge(h_hi_ready, (b - 1) * NJ + (arg + 1))
                    nc.gpsimd.tensor_tensor(h_lo[:, arg, :], h_sum[:, arg % 2, :], h_hi[:, arg, :].bitcast(F32),
                                            ALU.subtract).then_inc(h_ready, 1)

            def prologue():
                nc.gpsimd.memset(ident[:, :], 0.0).then_inc(zeroed, 1)
                nc.gpsimd.memset(rot[:, :, :], 0.0).then_inc(zeroed, 1)
                nc.gpsimd.memset(mask[:, :], 0.0).then_inc(zeroed, 1)
                nc.gpsimd.memset(mhalf[:, :], -0.5)
                nc.gpsimd.memset(y[:, :, :], 0.0).then_inc(y_free, 16)
                pool.wait_ge(zeroed, 3)
                nc.gpsimd.affine_select(out=ident[:, :], in_=ident[:, :], compare_op=ALU.not_equal, fill=1.0, base=0,
                                        pattern=[[-1, P]], channel_multiplier=1).then_inc(ident_ready, 1)
                half = ROPE // 2
                for k, (sign, base) in enumerate(((-1.0, -half), (1.0, 0))):
                    v = rot[:, :, k * half:(k + 1) * half]
                    nc.gpsimd.affine_select(out=v, in_=v, compare_op=ALU.not_equal, fill=sign, base=base,
                                            pattern=[[-ROPE, 2], [-1, half]], channel_multiplier=1)\
                        .then_inc(rot_ready, 1)
                nc.gpsimd.affine_select(out=mask[:, P:2 * P], in_=mask[:, P:2 * P], compare_op=ALU.is_ge, fill=MASKED,
                                        base=0, pattern=[[-1, P]], channel_multiplier=1).then_inc(mask_ready, 1)
                event("SQUARES", 0, "prologue", 0)
                c_split(0)
                for h in range(2):
                    normalise(0, 0, h)

            def step(b, s, ahead, behind, leave, left, part):
                if follows(b, s, 1):
                    normalise(*after(b, s, 1), 0)
                if left:
                    event(*left)
                if follows(b, s, 1):
                    normalise(*after(b, s, 1), 1)
                if s == LATE_SUM + 1 and part != "first":
                    o_split(b, LATE_SUM)
                if s == NP - 1 and follows(b, s, 1):
                    c_split(b + 1)
                for e in ahead:
                    event(*e)
                if s != LATE_SUM or part == "first":
                    o_split(b, s)
                for e in behind:
                    event(*e)

            def tile_rsqrt(i):
                for t in range(NT):
                    pool.wait_ge(tile_vareps, i * NT + t + 1)
                    nc.gpsimd.tensor_tensor(rstd[:, t:t + 1], vareps[:, t:t + 1], mhalf[:, t:t + 1], ALU.pow)\
                        .then_inc(tile_rstd, 1)

            def epilogue(events):
                tile_rsqrt(0)
                for e in events:
                    if e[0] == "GU":
                        event(*e)
                tile_rsqrt(1)

            run(pool, prologue, step, epilogue)


_INS = ["L0_attn_hidden_states", "L0_attn_Wq", "L0_attn_Wkva", "L0_attn_kv_a_norm_weight", "L0_attn_Wkvb",
        "L0_attn_Wo", "L0_attn_cos", "L0_attn_sin", "L0_ffn_w_gate", "L0_ffn_w_up", "L0_ffn_w_down"]


def kernel(**inputs):
    import numpy as _np
    import concourse.bacc as _bacc
    from concourse import mybir as _mybir
    from concourse.bass_utils import run_bass_kernel_spmd as _run

    nc = _bacc.Bacc("TRN2", target_bir_lowering=False, num_devices=1)
    arrays, args = {}, []
    for name in _INS:
        a = _np.ascontiguousarray(inputs[name])
        arrays[f"in_{name}_dram"] = a
        args.append(nc.dram_tensor(f"in_{name}_dram", a.shape, _mybir.dt.from_np(a.dtype), kind="ExternalInput").ap())
    out = nc.dram_tensor("out_dram", (NB, S, HID), _mybir.dt.float32, kind="ExternalOutput").ap()
    layer(nc, *args, out)
    return _run(nc, [arrays], core_ids=[0]).results[0]["out_dram"]
```
